# Optimizing a Trainium2 kernel written in Bass

```python
import numpy as np
import jax
import jax.numpy as jnp

def _softmax(x, axis=-1):
    return jax.nn.softmax(x, axis=axis)

def _gelu(x):
    return jax.nn.gelu(x, approximate=True)

def _silu(x):
    return jax.nn.silu(x)

def _sigmoid(x):
    return jax.nn.sigmoid(x)

def _layernorm(x, axis=-1, eps=1e-05):
    m = jnp.mean(x, axis=axis, keepdims=True)
    v = jnp.var(x, axis=axis, keepdims=True)
    return (x - m) / jnp.sqrt(v + eps)

def _scatter_add(tgt, idx, src, axis=0):
    return tgt.at[idx].add(src)

def _segment_sum(src, seg, n):
    return jax.ops.segment_sum(src, seg, n)
kernel_name = 'mk_seq_postln_d1_jaxref_r4_96e495'

def setup_inputs(seed: int=0):
    np.random.seed(seed)
    _w = jnp.asarray

    def _L0_attn_setup():
        import jax, jax.numpy as jnp
        import numpy as np
        B, T, HS = (2, 512, 256)
        QK, VD, NH = (256, 512, 8)
        HD_QK, HD_V = (QK // NH, VD // NH)
        SCALE_BASE = 512.0
        EPS = 1e-05

        def _xpos(q, k, offset=0):
            L, D = (q.shape[1], q.shape[-1])
            half = D // 2
            scale_vec = (jnp.arange(0, D, 2, dtype=jnp.float32) + 0.4 * D) / (1.4 * D)
            pos = jnp.arange(L + offset, dtype=jnp.float32)
            scale = scale_vec[None, :] ** (pos[:, None] / SCALE_BASE)
            inv_freq = 1.0 / 10000.0 ** (jnp.arange(half, dtype=jnp.float32) / half)
            sinus = pos[:, None] * inv_freq[None, :]
            sin, cos = (jnp.sin(sinus), jnp.cos(sinus))
            scale, sin, cos = (scale[-L:], sin[-L:], cos[-L:])

            def dup(m):
                return jnp.repeat(m, 2, axis=-1)

            def rot(x):
                x1, x2 = (x[..., ::2], x[..., 1::2])
                return jnp.stack((-x2, x1), axis=-1).reshape(x.shape)

            def apply(x, s):
                return x * dup(cos * s) + rot(x) * dup(sin * s)
            return (apply(q, scale), apply(k, 1.0 / scale))

        def _reference_tuple_inner(hidden_states, w_qkv, w_gated, w_proj, decay):
            Bsz, L, _ = hidden_states.shape
            qkv = hidden_states @ w_qkv.T
            q, k, v = (qkv[..., :QK], qkv[..., QK:2 * QK], qkv[..., 2 * QK:])
            q, k = _xpos(q, k)
            q = q.reshape(Bsz, L, NH, HD_QK).transpose(0, 2, 1, 3)
            k = k.reshape(Bsz, L, NH, HD_QK).transpose(0, 2, 1, 3)
            v = v.reshape(Bsz, L, NH, HD_V).transpose(0, 2, 1, 3)
            idx = jnp.arange(L)
            expo = idx[:, None] - idx[None, :]
            causal = expo >= 0
            dm = jnp.where(causal[None], decay[:, None, None] ** jnp.where(causal, expo, 0).astype(jnp.float32)[None], 0.0)
            scale = HD_QK ** (-0.5)
            retention = jnp.einsum('bhtd,bhsd->bhts', q, k) * scale * dm[None]
            out = jnp.einsum('bhts,bhsv->bhtv', retention, v)
            curr_kv = jnp.einsum('bhsd,bhsv,hs->bhdv', k, v, dm[:, -1, :])
            x = out.transpose(0, 2, 1, 3).reshape(Bsz, L, NH, HD_V)
            mu = x.mean(-1, keepdims=True)
            var = ((x - mu) ** 2).mean(-1, keepdims=True)
            normed = ((x - mu) / jnp.sqrt(var + EPS)).reshape(Bsz, L, VD)
            gate = jax.nn.silu(hidden_states @ w_gated.T)
            y = gate * normed @ w_proj.T
            return (y, curr_kv)
        key = jax.random.key(seed)
        ks = jax.random.split(key, 4)
        hidden_states = jax.random.normal(ks[0], (B, T, HS), dtype=jnp.float32)
        w_qkv = jax.random.normal(ks[1], (2 * QK + VD, HS), dtype=jnp.float32) * 0.02
        w_gated = jax.random.normal(ks[2], (VD, HS), dtype=jnp.float32) * 0.02
        w_proj = jax.random.normal(ks[3], (HS, VD), dtype=jnp.float32) * 0.02
        decay = jnp.asarray(1.0 - np.exp(np.linspace(np.log(1 / 32), np.log(1 / 128), NH)), dtype=jnp.float32)
        return {'hidden_states': hidden_states, 'w_qkv': w_qkv, 'w_gated': w_gated, 'w_proj': w_proj, 'decay': decay}
    _L0_attn_in = _L0_attn_setup()

    def _L0_ffn_setup():
        import jax, jax.numpy as jnp
        import numpy as np
        E = 8
        K = 2
        D = 256
        H = 1024
        CAP_FACTOR = 1.0
        key = jax.random.key(seed)
        ks = jax.random.split(key, 5)
        x = jax.random.normal(ks[0], (4, 512, D), jnp.float32)
        gate_w = jax.random.normal(ks[1], (E, D), jnp.float32) * 0.02
        fc1_w = jax.random.normal(ks[2], (E, H, D), jnp.float32) * 0.02
        fc1_b = jnp.zeros((E, 1, H), jnp.float32)
        fc2_w = jax.random.normal(ks[3], (E, H, D), jnp.float32) * 0.02
        fc2_b = jnp.zeros((E, 1, D), jnp.float32)
        return {'x': x, 'gate_w': gate_w, 'fc1_w': fc1_w, 'fc1_b': fc1_b, 'fc2_w': fc2_w, 'fc2_b': fc2_b}
    _L0_ffn_in = _L0_ffn_setup()
    _d = {'L0_attn_hidden_states': _L0_attn_in['hidden_states'], 'L0_attn_w_qkv': _L0_attn_in['w_qkv'], 'L0_attn_w_gated': _L0_attn_in['w_gated'], 'L0_attn_w_proj': _L0_attn_in['w_proj'], 'L0_attn_decay': _L0_attn_in['decay'], 'L0_ffn_gate_w': _L0_ffn_in['gate_w'], 'L0_ffn_fc1_w': _L0_ffn_in['fc1_w'], 'L0_ffn_fc1_b': _L0_ffn_in['fc1_b'], 'L0_ffn_fc2_w': _L0_ffn_in['fc2_w'], 'L0_ffn_fc2_b': _L0_ffn_in['fc2_b']}
    _x0 = _d['L0_attn_hidden_states']
    _d['L0_attn_hidden_states'] = jax.random.normal(jax.random.fold_in(jax.random.key(seed), 1), (8, 512, 256), dtype=_x0.dtype)
    del _x0
    return _d

def reference(L0_attn_hidden_states, L0_attn_w_qkv, L0_attn_w_gated, L0_attn_w_proj, L0_attn_decay, L0_ffn_gate_w, L0_ffn_fc1_w, L0_ffn_fc1_b, L0_ffn_fc2_w, L0_ffn_fc2_b):

    def _L0_attn_ref(hidden_states, w_qkv, w_gated, w_proj, decay):
        import jax, jax.numpy as jnp
        import numpy as np
        B, T, HS = (2, 512, 256)
        QK, VD, NH = (256, 512, 8)
        HD_QK, HD_V = (QK // NH, VD // NH)
        SCALE_BASE = 512.0
        EPS = 1e-05

        def _xpos(q, k, offset=0):
            L, D = (q.shape[1], q.shape[-1])
            half = D // 2
            scale_vec = (jnp.arange(0, D, 2, dtype=jnp.float32) + 0.4 * D) / (1.4 * D)
            pos = jnp.arange(L + offset, dtype=jnp.float32)
            scale = scale_vec[None, :] ** (pos[:, None] / SCALE_BASE)
            inv_freq = 1.0 / 10000.0 ** (jnp.arange(half, dtype=jnp.float32) / half)
            sinus = pos[:, None] * inv_freq[None, :]
            sin, cos = (jnp.sin(sinus), jnp.cos(sinus))
            scale, sin, cos = (scale[-L:], sin[-L:], cos[-L:])

            def dup(m):
                return jnp.repeat(m, 2, axis=-1)

            def rot(x):
                x1, x2 = (x[..., ::2], x[..., 1::2])
                return jnp.stack((-x2, x1), axis=-1).reshape(x.shape)

            def apply(x, s):
                return x * dup(cos * s) + rot(x) * dup(sin * s)
            return (apply(q, scale), apply(k, 1.0 / scale))

        def _reference_tuple_inner(hidden_states, w_qkv, w_gated, w_proj, decay):
            Bsz, L, _ = hidden_states.shape
            qkv = hidden_states @ w_qkv.T
            q, k, v = (qkv[..., :QK], qkv[..., QK:2 * QK], qkv[..., 2 * QK:])
            q, k = _xpos(q, k)
            q = q.reshape(Bsz, L, NH, HD_QK).transpose(0, 2, 1, 3)
            k = k.reshape(Bsz, L, NH, HD_QK).transpose(0, 2, 1, 3)
            v = v.reshape(Bsz, L, NH, HD_V).transpose(0, 2, 1, 3)
            idx = jnp.arange(L)
            expo = idx[:, None] - idx[None, :]
            causal = expo >= 0
            dm = jnp.where(causal[None], decay[:, None, None] ** jnp.where(causal, expo, 0).astype(jnp.float32)[None], 0.0)
            scale = HD_QK ** (-0.5)
            retention = jnp.einsum('bhtd,bhsd->bhts', q, k) * scale * dm[None]
            out = jnp.einsum('bhts,bhsv->bhtv', retention, v)
            curr_kv = jnp.einsum('bhsd,bhsv,hs->bhdv', k, v, dm[:, -1, :])
            x = out.transpose(0, 2, 1, 3).reshape(Bsz, L, NH, HD_V)
            mu = x.mean(-1, keepdims=True)
            var = ((x - mu) ** 2).mean(-1, keepdims=True)
            normed = ((x - mu) / jnp.sqrt(var + EPS)).reshape(Bsz, L, VD)
            gate = jax.nn.silu(hidden_states @ w_gated.T)
            y = gate * normed @ w_proj.T
            return (y, curr_kv)
        return _reference_tuple_inner(hidden_states, w_qkv, w_gated, w_proj, decay)[0]

    def _L0_ffn_ref(x, gate_w, fc1_w, fc1_b, fc2_w, fc2_b):
        import jax, jax.numpy as jnp
        import numpy as np
        E = 8
        K = 2
        D = 256
        H = 1024
        CAP_FACTOR = 1.0
        B, S, Dm = x.shape
        xf = x.reshape(-1, Dm)
        N = xf.shape[0]
        cap = int(K * CAP_FACTOR * ((N + E - 1) // E))
        logits = xf @ gate_w.T
        scores = jax.nn.softmax(logits, axis=-1)
        topv, topi = jax.lax.top_k(scores, K)
        gates = topv / jnp.sum(topv, axis=-1, keepdims=True)
        offset = jnp.zeros((E,), jnp.int32)
        locs = []
        for j in range(K):
            mask = jax.nn.one_hot(topi[:, j], E, dtype=jnp.int32)
            loc_in = jnp.cumsum(mask, axis=0) - 1 + offset[None, :]
            locs.append(jnp.take_along_axis(loc_in, topi[:, j:j + 1], axis=1)[:, 0])
            offset = offset + mask.sum(axis=0)
        loc = jnp.stack(locs, axis=1)
        valid = loc < cap
        flat_idx = jnp.where(valid, topi * cap + loc, 0)
        w = valid.astype(xf.dtype)
        disp = jnp.zeros((E * cap, Dm), xf.dtype)
        disp = disp.at[flat_idx.reshape(-1)].add((xf[:, None, :] * w[:, :, None]).reshape(-1, Dm))
        de = disp.reshape(E, cap, Dm)
        h = jax.nn.relu(jnp.einsum('ecd,ehd->ech', de, fc1_w) + fc1_b)
        eo = jnp.einsum('ech,ehd->ecd', h, fc2_w) + fc2_b
        gathered = eo.reshape(E * cap, Dm)[flat_idx]
        out = jnp.sum(gathered * (gates * w)[:, :, None], axis=1)
        return out.reshape(B, S, Dm)
    x = L0_attn_hidden_states
    x = _layernorm(x + _L0_attn_ref(x, L0_attn_w_qkv, L0_attn_w_gated, L0_attn_w_proj, L0_attn_decay), axis=-1)
    x = _layernorm(x + _L0_ffn_ref(x, L0_ffn_gate_w, L0_ffn_fc1_w, L0_ffn_fc1_b, L0_ffn_fc2_w, L0_ffn_fc2_b), axis=-1)
    return x

_drawn_inputs = setup_inputs


def setup_inputs(seed=0):
    import zlib

    import numpy as np

    out = dict(_drawn_inputs(seed))
    spreads = {'L0_ffn_fc1_b': (0.0, 0.1), 'L0_ffn_fc2_b': (0.0, 0.1)}
    factors = {}
    for name, (base, spread) in spreads.items():
        noise = np.random.default_rng([zlib.crc32(name.encode()), seed]).standard_normal(out[name].shape)
        drawn = base * np.exp(spread * noise) if base else spread * noise
        out[name] = jnp.asarray(drawn.astype(out[name].dtype))
    for name, factor in factors.items():
        out[name] = (out[name] * factor).astype(out[name].dtype)
    return out
```

```python
from contextlib import ExitStack

import numpy as np

import concourse.bass as bass
from concourse import mybir
from concourse.alu_op_type import AluOpType as ALU

F32 = mybir.dt.float32
F32R = mybir.dt.float32r
BF16 = mybir.dt.bfloat16
I32 = mybir.dt.int32
U32 = mybir.dt.uint32
ACT = mybir.ActivationFunctionType
AX = mybir.AxisListType.X

P = 128
B, T, D = 8, 512, 256
NH, DK, DV = 8, 32, 64
VD = NH * DV
NC = T // P
N = B * T
TILES = N // P
KD = D // P
E, H, TOPK = 8, 1024, 2
CAP = TOPK * N // E
SLOTS = E * CAP
HB = H // P
UT = 512
UM = UT // P
UNITS = SLOTS // UT
EPS = 1e-5
SKIP = 65536.0
LASTLAG = 4


def need(eng, sem, value):
    if not isinstance(value, int) or value > 0:
        eng.wait_ge(sem, value)


def hold(eng, sem, value, held):
    if not isinstance(value, int) or value > 0:
        eng.wait_ge(sem, value)
        eng.sem_inc(held, 1)


class Chunk:

    def __init__(self, b, c, lag=0):
        self.c = (c - lag) % NC
        self.b = b + (c - lag) // NC
        self.n = self.b * NC + self.c
        self.live = not isinstance(self.n, int) or 0 <= self.n < TILES
        self.par = self.c % 2

    def uses(self):
        return self.b * (NC // 2) + self.c // 2


def steps(eng, step, first=0):
    for c in range(NC):
        step(0, c)
    with eng.Fori(1, B - 1) as b:
        for c in range(NC):
            step(b, c)
    for c in range(NC):
        step(B - 1, c)
    for c in range(LASTLAG):
        step(B, c)


def moe_layer(nc, xT, xk, wT, wpT, decay, gwT, w1T, b1, w2, b2, rope, consts, out, dbg=None):
    with ExitStack() as top:
        def dram(name, shape, dt=F32):
            return nc.dram_tensor(name, shape, dt, kind="Internal").ap()

        def sem(name):
            return top.enter_context(nc.semaphore(name))

        def sb(name, shape, dt=F32, ctx=top):
            return ctx.enter_context(nc.sbuf_tensor(name, shape, dt))

        decay_rows = dram("decay_rows", [NH, 512])
        x1_rows = dram("x1_rows", [N, D])
        slot_ids = dram("slot_ids", [TOPK * SLOTS, 1])
        y_rows = dram("y_rows", [TOPK * N, D])

        x1_all = sb("x1_all", [P, TILES, D])
        top_all = sb("top_all", [P, TILES, 2])
        pick_all = sb("pick_all", [P, TILES, 4])
        count = sb("count", [P, TOPK * E])
        const = sb("const", [P, consts.shape[1]])
        ident = const[:, 0:128]
        iota8 = const[:, 256:272].rearrange("p (j e) -> p j e", e=E)
        sign2 = const[:, 272:274]
        off2 = const[:, 274:276]
        token0 = const[:, 276:284].rearrange("p (c j) -> p c j", j=2)
        slot_no = const[:, 284:348].rearrange("p (e k) -> p e k", e=E)

        phase_one(nc, top, sem, sb, locals())
        phase_two(nc, top, sem, sb, locals())


def phase_one(nc, top, sem, sb_, v):
    xT, xk, wT, wpT, decay, gwT = (v[k] for k in ("xT", "xk", "wT", "wpT", "decay", "gwT"))
    rope, consts = v["rope"], v["consts"]
    decay_rows, x1_rows, slot_ids, y_rows = (v[k] for k in ("decay_rows", "x1_rows", "slot_ids", "y_rows"))
    x1_all, top_all, pick_all, count, const = (v[k] for k in ("x1_all", "top_all", "pick_all", "count", "const"))
    ident, iota8, sign2, off2, token0 = (v[k] for k in ("ident", "iota8", "sign2", "off2", "token0"))
    before = const[:, 128:256]

    with ExitStack() as ctx:
        def sb(name, shape, dt=F32):
            return ctx.enter_context(nc.sbuf_tensor(name, shape, dt))

        def psum(name, shape):
            return ctx.enter_context(nc.psum_tensor(name, shape, F32))

        W3 = 2 * D + 2 * VD
        w_hi, w_lo = (sb(f"w_{x}", [P, KD, W3], F32R) for x in ("hi", "lo"))
        wp_hi, wp_lo = (sb(f"wp_{x}", [P, VD // P, D], F32R) for x in ("hi", "lo"))
        raw = x1_all[:, :, :].rearrange("p t d -> p (t d)")
        w_raw = raw[:, 0:KD * W3].rearrange("p (k n) -> p k n", k=KD)
        wp_raw = raw[:, KD * W3:KD * W3 + VD * 2].rearrange("p (k n) -> p k n", n=D)
        gw = sb("gw", [P, KD, 96])
        cos_t = sb("cos_t", [P, NC, 2 * D])
        sin_t = sb("sin_t", [P, NC, 2 * D])
        drow = sb("drow", [NH, 512])
        dpow = sb("dpow", [NH, 8])
        fade = sb("fade", [P, NH, P])
        fade_q = sb("fade_q", [P, 2, P])
        fade_k = fade[:, :, P - 1:P]
        fade_c = fade_q[:, :, P - 1]
        vmean = sb("vmean", [P, KD, NH])
        before_b = sb("before_b", [P, P], BF16)
        ones_b = sb("ones_b", [P, P], BF16)
        half_neg = sb("half_neg", [P, NH])
        token = sb("token", [P, NC, 2])
        zeros = sb("zeros", [P, 1024])

        xt_raw = sb("xt_raw", [P, NC, KD, P])
        xt_hi, xt_lo = (sb(f"xt_{x}", [P, NC, KD, P], F32R) for x in ("hi", "lo"))
        x_tok = sb("x_tok", [P, NC, D])
        rot_a = sb("rot_a", [P, 2 * D])
        rot_b = sb("rot_b", [P, 2 * D])
        qk = sb("qk", [P, 2, 2 * D])
        k_fade = sb("k_fade", [P, 2, D])
        k_t = sb("k_t", [P, 2, 2, P])
        q_diag = sb("q_diag", [P, 2, 2, 4, P])
        q_fade = sb("q_fade", [P, 2, 2, P])
        v_pad = sb("v_pad", [P, 2, NH, P])
        probs = sb("probs", [P, 2, NH, P])
        gate = sb("gate", [P, 2, VD])
        state = sb("state", [P, 2, 2, 4 * DV])
        square = sb("square", [P, VD])
        ssum = sb("ssum", [P, 2, NH])
        svar = sb("svar", [P, NH])
        srstd = sb("srstd", [P, 2, NH])
        normed = sb("normed", [P, VD])
        gated = sb("gated", [P, 2, VD])
        gt_hi, gt_lo = (sb(f"gt_{x}", [P, VD // P, P], F32R) for x in ("hi", "lo"))
        z = sb("z", [P, 2, D])
        zstat = sb("zstat", [P, 2, 6])
        zmean = sb("zmean", [P, 2, 2])
        zvar = sb("zvar", [P, 1])
        zrstd = sb("zrstd", [P, 2, 1])
        x1 = sb("x1", [P, 2, D])
        x1_t = sb("x1_t", [P, KD, P])
        logit = sb("logit", [P, E])
        best = sb("best", [P, 8])
        besti = sb("besti", [P, 8], U32)
        pick = sb("pick", [P, 2, 4])
        hot = sb("hot", [P, TOPK * E], BF16)
        place = sb("place", [P, TOPK * E])
        over = sb("over", [P, 2])
        sbase = sb("sbase", [P, 2])
        splace = sb("splace", [P, 2])
        slot_f = sb("slot_f", [P, 2])
        slot = sb("slot", [P, 2, 2], I32)

        ps_qk = psum("ps_qk", [P, 512])
        ps_v = psum("ps_v", [P, 512])
        ps_g = psum("ps_g", [P, 512])
        ps_t = psum("ps_t", [P, 512])
        ps_s = psum("ps_s", [P, 1024])
        ps_o = psum("ps_o", [P, 512])
        ps_y = psum("ps_y", [P, 512])

        names = """w_in const_in rope_in decay_in drow_out fades_in fade_set gw_in ids_set y_zeroed
        centred w_split_hi w_split_lo drow_ready fixed small_set zero_set
        qk_done v_done g_done t_done s_done o_done u_done n_done y_done xt_done l_done c_done
        xhi_done v_out gate_done t_out square_done ghi_done x1t_out
        xlo_done rotated qfade_done probs_done state_done ssum_done normed_done gated_done glo_done z_done
        zstat_done zmean_done x1_done logit_out best_done besti_done pick_set hot_done place_sum place_mul
        place_done count_done kept
        setup_step dve_held pool_held qk_sum kfade_done svar_done srstd_done zvar_done zrstd_done over_done sb1 sb2 sp1 sb3 slot_sum slot_done token_set""".split()
        s = {k: sem(k) for k in names}
        xt_in = [sem(f"xt_in{c}") for c in range(NC)]
        xk_in = [sem(f"xk_in{c}") for c in range(NC)]
        x1_saved = [sem(f"x1_saved{c}") for c in range(2)]
        ids_sent = [sem(f"ids_sent{c}") for c in range(NC)]

        block = ctx.enter_context(nc.Block())

        @block.sync
        def _(sp):
            def load_columns(m):
                need(sp, s["xlo_done"], m.n - NC + 1)
                sp.dma_start(xt_raw[:, m.c], xT[:, :, bass.ds(m.n * P, P)]).then_inc(xt_in[m.c], 16)

            def load_rows(m):
                need(sp, s["z_done"], m.n - NC + 1)
                sp.dma_start(x_tok[:, m.c, :], xk[bass.ds(m.n * P, P), :]).then_inc(xk_in[m.c], 16)

            sp.dma_start(w_raw, wT).then_inc(s["w_in"], 16)
            sp.dma_start(wp_raw, wpT).then_inc(s["w_in"], 16)
            sp.dma_start(dpow[:, 0:1], decay).then_inc(s["decay_in"], 16)
            sp.dma_start(const[:, :], consts).then_inc(s["const_in"], 16)
            sp.dma_start(gw[:, :, 0:E], gwT).then_inc(s["gw_in"], 16)
            for c in range(NC):
                load_columns(Chunk(0, c))
            for c in range(NC):
                load_rows(Chunk(0, c))
            sp.dma_start(cos_t[:, :, :], rope[0]).then_inc(s["rope_in"], 16)
            sp.dma_start(sin_t[:, :, :], rope[1]).then_inc(s["rope_in"], 16)
            sp.wait_ge(s["drow_ready"], 1)
            sp.dma_start(decay_rows, drow[:, :]).then_inc(s["drow_out"], 16)
            sp.wait_ge(s["drow_out"], 16)
            rows = decay_rows.tensor
            sp.dma_start(probs[:, 0], bass.AP(rows, 257, [[1, P], [512, NH], [1, P]])).then_inc(s["fades_in"], 16)
            for j in range(4):
                sp.dma_start(fade_q[DK * j:DK * j + DK, :, :],
                             bass.AP(rows, 512 * j + 128, [[0, DK], [2048, 2], [1, P]])).then_inc(s["fades_in"], 16)
            sp.wait_ge(s["zero_set"], 2)
            sp.dma_start(slot_ids.rearrange("(p c) o -> p (c o)", p=P), zeros[:, 0:P]).then_inc(s["ids_set"], 16)

            def step(b, c):
                m = Chunk(b + 1, c)
                if m.live and Chunk(b, c).live:
                    load_columns(m)
                m = Chunk(b, c, 2)
                if m.live:
                    if isinstance(m.n, int) and m.n == 0:
                        sp.wait_ge(s["w_split_lo"], 1)
                    sp.wait_ge(s["x1_done"], m.n + 1)
                    sp.dma_start(x1_all[:, bass.ds(m.n, 1), :].rearrange("p a d -> p (a d)"), x1[:, m.par, :])\
                      .then_inc(x1_saved[m.par], 16)
                    sp.dma_start(x1_rows[bass.ds(m.n * P, P), :], x1[:, m.par, :]).then_inc(x1_saved[m.par], 16)
                    m = Chunk(m.b + 1, m.c)
                    if m.live:
                        load_rows(m)

            steps(sp, step)
            for k in range(2):
                sp.wait_ge(x1_saved[k], 32 * TILES // 2)

        @block.scalar
        def _(act):
            def split_x(m):
                act.wait_ge(xt_in[m.c], (m.b + 1) * 16)
                need(act, s["g_done"], m.n - NC + 1)
                act.activation(xt_hi[:, m.c], xt_raw[:, m.c], ACT.Copy).then_inc(s["xhi_done"], 1)

            act.wait_ge(s["w_in"], 32)
            act.activation(wp_hi[:, :, :], wp_raw, ACT.Copy).then_inc(s["w_split_hi"], 1)
            act.wait_ge(s["centred"], 1)
            for k in range(KD):
                act.activation(w_hi[:, k, :], w_raw[:, k, :], ACT.Copy).then_inc(s["w_split_hi"], 1)
            for c in range(NC):
                split_x(Chunk(0, c))
            act.wait_ge(s["small_set"], 4)

            def step(b, c):
                m = Chunk(b, c, 1)
                if m.live:
                    act.wait_ge(s["o_done"], m.n + 1)
                    need(act, s["ssum_done"], m.n)
                    act.activation(square[:, :], ps_o[:, :], ACT.Square).then_inc(s["square_done"], 1)
                m = Chunk(b, c)
                if m.live:
                    act.wait_ge(s["v_done"], m.n + 1)
                    need(act, s["o_done"], m.n - 1)
                    vv = v_pad[:, m.par].rearrange("p (a two) (f c) -> p a (two f) c", two=2, c=DV)
                    act.activation(vv[:, :, ::3, :], ps_v[:, :].rearrange("p (a f c) -> p a f c", f=2, c=DV), ACT.Copy)\
                       .then_inc(s["v_out"], 1)
                    act.wait_ge(s["t_done"], m.n + 1)
                    need(act, s["s_done"], m.n - 1)
                    act.activation(k_t[:, m.par], ps_t[:, 2 * P:4 * P].rearrange("p (g t) -> p g t", g=2), ACT.Copy)
                    for j in range(4):
                        r = slice(DK * j, DK * j + DK)
                        o = act.activation(q_diag[r, m.par, :, j, :],
                                           ps_t[r, 0:2 * P].rearrange("p (g t) -> p g t", g=2), ACT.Copy)
                    o.then_inc(s["t_out"], 1)
                    act.wait_ge(s["g_done"], m.n + 1)
                    need(act, s["gated_done"], m.n - 1)
                    act.activation(gate[:, m.par, :], ps_g[:, :], ACT.Silu).then_inc(s["gate_done"], 1)
                m = Chunk(b, c, 1)
                if m.live:
                    act.wait_ge(s["n_done"], m.n + 1)
                    need(act, s["y_done"], m.n)
                    act.activation(gt_hi[:, :, :].rearrange("p k t -> p (k t)"), ps_t[:, :], ACT.Copy)\
                       .then_inc(s["ghi_done"], 1)
                m = Chunk(b, c, 3)
                if m.live:
                    act.wait_ge(s["xt_done"], m.n + 1)
                    need(act, s["l_done"], m.n)
                    act.activation(x1_t[:, :, :].rearrange("p k t -> p (k t)"), ps_y[:, 0:D], ACT.Copy)\
                       .then_inc(s["x1t_out"], 1)
                m = Chunk(b + 1, c)
                if m.live and Chunk(b, c).live:
                    split_x(m)

            steps(act, step)

        @block.tensor
        def _(pe):
            for k in ("const_in", "gw_in"):
                pe.wait_ge(s[k], 16)
            pe.wait_ge(s["small_set"], 4)
            pe.wait_ge(s["fixed"], 1)
            pe.wait_ge(s["w_split_hi"], 3)
            pe.wait_ge(s["w_split_lo"], 1)

            def three(out_, a_hi, a_lo, b_hi, b_lo, last, first=True):
                pe.matmul(out_, a_hi, b_hi, start=first, stop=False)
                pe.matmul(out_, a_hi, b_lo, start=False, stop=False)
                return pe.matmul(out_, a_lo, b_hi, start=False, stop=last)

            def project(out_, m, col):
                for k in range(KD):
                    o = three(out_, xt_hi[:, m.c, k, :], xt_lo[:, m.c, k, :], w_hi[:, k, col:col + 512],
                              w_lo[:, k, col:col + 512], k == KD - 1, k == 0)
                return o

            def step(b, c):
                m0, m1, m2, m3, m4 = (Chunk(b, c, lag) for lag in range(5))
                if m0.live:
                    pe.wait_ge(s["xlo_done"], m0.n + 1)
                    need(pe, s["rotated"], 2 * m0.n)
                    project(ps_qk[:, :], m0, 0).then_inc(s["qk_done"], 1)
                if m4.live:
                    pe.wait_ge(s["x1t_out"], m4.n + 1)
                    for k in range(KD):
                        o = pe.matmul(ps_y[:, 256:352], x1_t[:, k, :], gw[:, k, :], start=k == 0, stop=k == KD - 1)
                    o.then_inc(s["l_done"], 1)
                if m1.live:
                    need(pe, s["normed_done"], m1.n)
                    pe.wait_ge(s["probs_done"], m1.n + 1)
                    pe.wait_ge(s["v_out"], m1.n + 1)
                    if m1.c > 0:
                        pe.wait_ge(s["qfade_done"], m1.n + 1)
                        pe.wait_ge(s["state_done"], m1.b * (NC - 1) + m1.c)
                        for g in range(2):
                            pe.matmul(ps_o[:, 256 * g:256 * g + 256], q_fade[:, m1.par, g, :], state[:, m1.par, g, :],
                                      start=g == 0, stop=False, skip_group_check=True)
                    for h in range(NH):
                        pair = h // 2
                        o = pe.matmul(ps_o[:, P * pair:P * pair + P], probs[:, m1.par, h, :], v_pad[:, m1.par, h, :],
                                      start=(m1.c == 0 and h == 0), stop=(h == NH - 1), skip_group_check=True)
                    o.then_inc(s["o_done"], 1)
                if m0.live:
                    full = m0.b * (NC - 1) + min(m0.c, NC - 1)
                    need(pe, s["state_done"], full)
                    need(pe, s["v_out"], m0.n)
                    project(ps_v[:, :], m0, 2 * D).then_inc(s["v_done"], 1)
                    pe.wait_ge(s["qk_sum"], m0.n + 1)
                    need(pe, s["glo_done"], m0.n - 1)
                    need(pe, s["qfade_done"], m0.n)
                    for i in range(4):
                        o = pe.transpose(ps_t[:, P * i:P * i + P], qk[:, m0.par, P * i:P * i + P], ident)
                    o.then_inc(s["t_done"], 1)
                    need(pe, s["gate_done"], m0.n)
                    project(ps_g[:, :], m0, 2 * D + VD).then_inc(s["g_done"], 1)
                if m2.live:
                    pe.wait_ge(s["glo_done"], m2.n + 1)
                    need(pe, s["logit_out"], m2.n - 1)
                    need(pe, s["x1t_out"], m2.n - 1)
                    for k in range(VD // P):
                        o = three(ps_y[:, 0:D], gt_hi[:, k, :], gt_lo[:, k, :], wp_hi[:, k, :], wp_lo[:, k, :],
                                  k == VD // P - 1, k == 0)
                    o.then_inc(s["y_done"], 1)
                if m0.live:
                    pe.wait_ge(s["t_out"], m0.n + 1)
                    need(pe, s["probs_done"], m0.n)
                    for g in range(2):
                        o = pe.matmul(ps_s[:, 512 * g:512 * g + 512], k_t[:, m0.par, g, :],
                                      q_diag[:, m0.par, g].rearrange("p j t -> p (j t)"), start=True, stop=True)
                    o.then_inc(s["s_done"], 1)
                if m4.live:
                    pe.wait_ge(s["hot_done"], m4.n + 1)
                    if m2.live:
                        pe.wait_ge(s["z_done"], m2.n + 1)
                    pe.matmul(ps_y[:, 384:400], before_b[:, :], hot[:, :], start=True, stop=True)
                    pe.matmul(ps_y[:, 400:416], ones_b[:, :], hot[:, :], start=True, stop=True)\
                      .then_inc(s["c_done"], 1)
                if m0.live and m0.c < NC - 1:
                    pe.wait_ge(s["kfade_done"], m0.b * (NC - 1) + m0.c + 1)
                    pe.wait_ge(s["v_out"], m0.n + 1)
                    for g in range(2):
                        vg = v_pad[:, m0.par].rearrange("p (a two) (f c) -> p a (two f) c", two=2, c=DV)
                        vg = vg[:, 2 * g:2 * g + 2, ::3, :]
                        o = pe.matmul(ps_v[:, 256 * g:256 * g + 256], k_fade[:, m0.par, P * g:P * g + P],
                                      vg, start=True, stop=True)
                    o.then_inc(s["u_done"], 1)
                if m1.live:
                    pe.wait_ge(s["gated_done"], m1.n + 1)
                    if m0.live:
                        pe.wait_ge(s["qfade_done"], m0.n + 1)
                    for i in range(4):
                        o = pe.transpose(ps_t[:, P * i:P * i + P], gated[:, m1.par, P * i:P * i + P], ident)
                    o.then_inc(s["n_done"], 1)
                if m3.live:
                    pe.wait_ge(s["x1_done"], m3.n + 1)
                    need(pe, s["count_done"], m3.n)
                    if m2.live:
                        pe.wait_ge(s["z_done"], m2.n + 1)
                    for k in range(KD):
                        o = pe.transpose(ps_y[:, P * k:P * k + P], x1[:, m3.par, P * k:P * k + P], ident)
                    o.then_inc(s["xt_done"], 1)

            steps(pe, step)

        @block.vector
        def _(dve):
            def split_x(m):
                dve.wait_ge(s["xhi_done"], m.n + 1)
                dve.tensor_tensor(xt_lo[:, m.c], xt_raw[:, m.c], xt_hi[:, m.c].bitcast(F32), ALU.subtract)\
                   .then_inc(s["xlo_done"], 1)

            passed = [0]

            def chain(instruction):
                instruction.then_inc(s["setup_step"], 1)
                passed[0] += 1
                dve.wait_ge(s["setup_step"], passed[0])

            chain(dve.memset(drow[:, :], 0.0))
            chain(dve.memset(drow[:, 127:128], 1.0))
            dve.wait_ge(s["decay_in"], 16)
            for i in range(7):
                chain(dve.tensor_tensor(dpow[:, i + 1:i + 2], dpow[:, i:i + 1], dpow[:, i:i + 1], ALU.mult))
            for i in range(7):
                w = 1 << i
                chain(dve.tensor_scalar(drow[:, 127 + w:127 + 2 * w], drow[:, 127:127 + w], dpow[:, i:i + 1],
                                             None, ALU.mult))
            chain(dve.tensor_copy(drow[:, 255:256], dpow[:, 7:8]))
            dve.tensor_copy(drow[:, 256:512], drow[:, 0:256][:, ::-1]).then_inc(s["drow_ready"], 1)
            dve.wait_ge(s["w_in"], 32)
            wv = [w_raw[:, k, 2 * D:2 * D + VD].rearrange("p (h c) -> p h c", h=NH) for k in range(KD)]
            for k in range(KD):
                chain(dve.tensor_reduce(vmean[:, k, :], wv[k], AX, ALU.add))
            chain(dve.tensor_scalar(vmean[:, :, :], vmean[:, :, :], 1.0 / DV, None, ALU.mult))
            for k in range(KD):
                o = dve.tensor_tensor(wv[k], wv[k], vmean[:, k, :].unsqueeze(2).to_broadcast([P, NH, DV]), ALU.subtract)
            o.then_inc(s["centred"], 1)
            dve.memset(q_diag[:, :, :, :, :], 0.0).then_inc(s["small_set"], 1)
            dve.memset(v_pad[:, :, :, :], 0.0).then_inc(s["small_set"], 1)
            dve.memset(state[:, :, :, :], 0.0).then_inc(s["small_set"], 1)
            dve.memset(gw[:, :, E:96], 0.0).then_inc(s["small_set"], 1)
            dve.wait_ge(s["const_in"], 16)
            dve.memset(ones_b[:, :], 1.0)
            dve.memset(count[:, :], 0.0)
            dve.tensor_copy(before_b[:, :], before).then_inc(s["fixed"], 1)
            dve.wait_ge(s["w_split_hi"], 3)
            dve.wait_ge(s["centred"], 1)
            for k in range(KD):
                dve.tensor_tensor(w_lo[:, k, :], w_raw[:, k, :], w_hi[:, k, :].bitcast(F32), ALU.subtract)
            dve.tensor_tensor(wp_lo[:, :, :], wp_raw, wp_hi[:, :, :].bitcast(F32), ALU.subtract)\
               .then_inc(s["w_split_lo"], 1)
            for c in range(NC):
                split_x(Chunk(0, c))
            dve.wait_ge(s["rope_in"], 32)
            dve.wait_ge(s["fades_in"], 16 * 5)
            dve.tensor_copy(fade[:, :, :], probs[:, 0, :, ::-1]).then_inc(s["fade_set"], 1)
            dve.wait_ge(s["fade_set"], 1)
            dve.wait_ge(s["small_set"], 4)

            def step(b, c):
                m0, m1, m2, m3, m4 = (Chunk(b, c, lag) for lag in range(5))
                if m0.live:
                    dve.wait_ge(s["qk_done"], m0.n + 1)
                    need(dve, s["qk_sum"], m0.n)
                    dve.tensor_tensor(rot_a[:, :], ps_qk[:, :], cos_t[:, m0.c, :], ALU.mult).then_inc(s["rotated"], 1)
                    pairs = [t.rearrange("p (f two) -> p f two", two=2)
                             for t in (rot_b[:, :], ps_qk[:, :], sin_t[:, m0.c, :])]
                    dve.tensor_tensor(pairs[0], pairs[1][:, :, ::-1], pairs[2], ALU.mult).then_inc(s["rotated"], 1)
                if m4.live:
                    dve.wait_ge(s["l_done"], m4.n + 1)
                    dve.tensor_copy(logit[:, :], ps_y[:, 256:256 + E]).then_inc(s["logit_out"], 1)
                    hold(dve, s["logit_out"], m4.n + 1, s["dve_held"])
                    dve.max(best[:, :], logit[:, :]).then_inc(s["best_done"], 1)
                    hold(dve, s["best_done"], m4.n + 1, s["dve_held"])
                    dve.max_index(besti[:, :], best[:, :], logit[:, :]).then_inc(s["besti_done"], 1)
                    dve.tensor_copy(top_all[:, bass.ds(m4.n, 1), :].rearrange("p a j -> p (a j)"), best[:, 0:2])
                    dve.wait_ge(s["besti_done"], m4.n + 1)
                    need(dve, s["slot_done"], m4.n)
                    dve.tensor_copy(pick[:, m4.par, 0:2], besti[:, 0:2]).then_inc(s["pick_set"], 1)
                    dve.wait_ge(s["pick_set"], m4.n + 1)
                    need(dve, s["c_done"], m4.n)
                    dve.tensor_tensor(hot[:, :].rearrange("p (j e) -> p j e", e=E), iota8,
                                      pick[:, m4.par, 0:2].unsqueeze(2).to_broadcast([P, 2, E]), ALU.is_equal)\
                       .then_inc(s["hot_done"], 1)
                if m1.live:
                    dve.wait_ge(s["square_done"], m1.n + 1)
                    need(dve, s["svar_done"], m1.n - 1)
                    dve.tensor_reduce(ssum[:, m1.par, :], square[:, :].rearrange("p (h c) -> p h c", h=NH), AX, ALU.add)\
                       .then_inc(s["ssum_done"], 1)
                if m0.live:
                    dve.wait_ge(s["t_out"], m0.n + 1)
                    need(dve, s["o_done"], m0.n - 1)
                    dve.tensor_tensor(q_fade[:, m0.par].rearrange("p g t -> p (g t)"), ps_t[:, 0:2 * P],
                                      fade_q[:, :, :].rearrange("p g t -> p (g t)"), ALU.mult)\
                       .then_inc(s["qfade_done"], 1)
                if m1.live:
                    dve.wait_ge(s["srstd_done"], m1.n + 1)
                    need(dve, s["gated_done"], m1.n)
                    dve.tensor_tensor(normed[:, :].rearrange("p (h c) -> p h c", h=NH),
                                      ps_o[:, :].rearrange("p (h c) -> p h c", h=NH),
                                      srstd[:, m1.par, :].unsqueeze(2).to_broadcast([P, NH, DV]), ALU.mult)\
                       .then_inc(s["normed_done"], 1)
                    dve.wait_ge(s["normed_done"], m1.n + 1)
                    dve.wait_ge(s["gate_done"], m1.n + 1)
                    need(dve, s["n_done"], m1.n - 1)
                    dve.tensor_tensor(gated[:, m1.par, :], normed[:, :], gate[:, m1.par, :], ALU.mult)\
                       .then_inc(s["gated_done"], 1)
                if m2.live:
                    dve.wait_ge(s["y_done"], m2.n + 1)
                    dve.wait_ge(xk_in[m2.c], (m2.b + 1) * 16)
                    dve.tensor_tensor(z[:, m2.par, :], ps_y[:, 0:D], x_tok[:, m2.c, :], ALU.add)\
                       .then_inc(s["z_done"], 1)
                    dve.wait_ge(s["z_done"], m2.n + 1)
                    dve.bn_stats(zstat[:, m2.par, :], z[:, m2.par, :]).then_inc(s["zstat_done"], 1)
                    hold(dve, s["zstat_done"], m2.n + 1, s["dve_held"])
                    dve.bn_aggr(zmean[:, m2.par, :], zstat[:, m2.par, :]).then_inc(s["zmean_done"], 1)
                if m0.live:
                    dve.wait_ge(s["s_done"], m0.n + 1)
                    need(dve, s["o_done"], m0.n - 1)
                    dve.tensor_tensor(probs[:, m0.par].rearrange("p h t -> p (h t)"), ps_s[:, :],
                                      fade[:, :, :].rearrange("p h t -> p (h t)"), ALU.mult)\
                       .then_inc(s["probs_done"], 1)
                if m4.live:
                    dve.wait_ge(s["c_done"], m4.n + 1)
                    need(dve, s["count_done"], m4.n)
                    dve.tensor_tensor(place[:, :], ps_y[:, 384:400], count[:, :], ALU.add).then_inc(s["place_sum"], 1)
                    dve.wait_ge(s["place_sum"], m4.n + 1)
                    dve.tensor_tensor(count[:, :], ps_y[:, 400:416], count[:, :], ALU.add).then_inc(s["count_done"], 1)
                    dve.tensor_tensor(place[:, :], place[:, :], hot[:, :], ALU.mult).then_inc(s["place_mul"], 1)
                    dve.wait_ge(s["place_mul"], m4.n + 1)
                    dve.tensor_reduce(pick[:, m4.par, 2:4], place[:, :].rearrange("p (j e) -> p j e", e=E), AX, ALU.add)\
                       .then_inc(s["place_done"], 1)
                    hold(dve, s["place_done"], m4.n + 1, s["dve_held"])
                    dve.tensor_copy(pick_all[:, bass.ds(m4.n, 1), :].rearrange("p a j -> p (a j)"), pick[:, m4.par, :])\
                       .then_inc(s["kept"], 1)
                if m0.live and m0.c < NC - 1:
                    dve.wait_ge(s["u_done"], m0.b * (NC - 1) + m0.c + 1)
                    need(dve, s["o_done"], m0.n)
                    if m0.c > 0:
                        dve.wait_ge(s["state_done"], m0.b * (NC - 1) + m0.c)
                    new, old = state[:, 1 - m0.par], state[:, m0.par]
                    for j in range(4):
                        r, col = slice(DK * j, DK * j + DK), slice(DV * j, DV * j + DV)
                        part = ps_v[r, :].rearrange("p (g c) -> p g c", g=2)[:, :, col]
                        if m0.c == 0:
                            o = dve.tensor_copy(new[r, :, col], part)
                        else:
                            for g in range(2):
                                o = dve.scalar_tensor_tensor(new[r, g, col], old[r, g, col], fade_c[r, g:g + 1],
                                                             part[:, g, :], ALU.mult, ALU.add)
                    o.then_inc(s["state_done"], 1)
                if m2.live:
                    dve.wait_ge(s["zrstd_done"], m2.n + 1)
                    need(dve, x1_saved[m2.par], m2.uses() * 32)
                    need(dve, s["xt_done"], m2.n - 1)
                    dve.tensor_scalar(x1[:, m2.par, :], z[:, m2.par, :], zmean[:, m2.par, 0:1], zrstd[:, m2.par, :],
                                      ALU.subtract, ALU.mult).then_inc(s["x1_done"], 1)
                if m1.live:
                    dve.wait_ge(s["ghi_done"], m1.n + 1)
                    dve.tensor_tensor(gt_lo[:, :, :].rearrange("p k t -> p (k t)"), ps_t[:, :],
                                      gt_hi[:, :, :].bitcast(F32).rearrange("p k t -> p (k t)"), ALU.subtract)\
                       .then_inc(s["glo_done"], 1)
                ahead = Chunk(b + 1, c)
                if ahead.live and m0.live:
                    split_x(ahead)

            steps(dve, step)

        @block.gpsimd
        def _(pool):
            pool.memset(zeros[:, :], float(TOPK * N)).then_inc(s["zero_set"], 1)
            pool.memset(half_neg[:, :], -0.5).then_inc(s["zero_set"], 1)
            pool.wait_ge(s["const_in"], 16)
            pool.wait_ge(s["zero_set"], 2)
            pool.tensor_copy(token[:, :, :], token0).then_inc(s["zero_set"], 1)
            pool.wait_ge(s["zero_set"], 3)
            pool.wait_ge(s["ids_set"], 16)
            pool.memset(zeros[:, :], 0.0).then_inc(s["zero_set"], 1)
            pool.wait_ge(s["zero_set"], 4)
            yz = y_rows.rearrange("(p a) d -> p (a d)", p=P)
            for i in range(TOPK * N * D // P // 1024):
                pool.dma_start(yz[:, 1024 * i:1024 * i + 1024], zeros[:, :]).then_inc(s["y_zeroed"], 16)
            pool.wait_ge(s["fade_set"], 1)

            def step(b, c):
                m0, m1, m2, m3, m4 = (Chunk(b, c, lag) for lag in range(5))
                if m0.live:
                    need(pool, s["t_done"], m0.n - 1)
                    pool.wait_ge(s["rotated"], 2 * m0.n + 2)
                    pool.tensor_tensor(qk[:, m0.par, :], rot_a[:, :], rot_b[:, :], ALU.add).then_inc(s["qk_sum"], 1)
                if m1.live:
                    hold(pool, s["ssum_done"], m1.n + 1, s["pool_held"])
                    pool.tensor_scalar(svar[:, :], ssum[:, m1.par, :], 1.0 / DV, EPS, ALU.mult, ALU.add)\
                        .then_inc(s["svar_done"], 1)
                    need(pool, s["normed_done"], m1.n - 1)
                    pool.wait_ge(s["svar_done"], m1.n + 1)
                    pool.tensor_tensor(srstd[:, m1.par, :], svar[:, :], half_neg[:, :], ALU.pow)\
                        .then_inc(s["srstd_done"], 1)
                if m0.live and m0.c < NC - 1:
                    need(pool, s["u_done"], m0.b * (NC - 1) + max(m0.c - 1, 0))
                    pool.wait_ge(s["qk_sum"], m0.n + 1)
                    pool.tensor_tensor(k_fade[:, m0.par].rearrange("p (h c) -> p h c", h=NH),
                                       qk[:, m0.par, D:2 * D].rearrange("p (h c) -> p h c", h=NH),
                                       fade_k.to_broadcast([P, NH, DK]), ALU.mult)\
                        .then_inc(s["kfade_done"], 1)
                if m2.live:
                    hold(pool, s["zmean_done"], m2.n + 1, s["pool_held"])
                    pool.tensor_scalar(zvar[:, :], zmean[:, m2.par, 1:2], EPS, None, ALU.add).then_inc(s["zvar_done"], 1)
                    need(pool, s["x1_done"], m2.n - 1)
                    pool.wait_ge(s["zvar_done"], m2.n + 1)
                    pool.tensor_tensor(zrstd[:, m2.par, :], zvar[:, :], half_neg[:, 0:1], ALU.pow)\
                        .then_inc(s["zrstd_done"], 1)
                if m4.live:
                    hold(pool, s["place_done"], m4.n + 1, s["pool_held"])
                    pool.tensor_scalar(over[:, :], pick[:, m4.par, 2:4], float(CAP), SKIP, ALU.is_ge, ALU.mult)\
                        .then_inc(s["over_done"], 1)
                    pool.tensor_scalar(sbase[:, :], pick[:, m4.par, 0:2], float(CAP), None, ALU.mult)\
                        .then_inc(s["sb1"], 1)
                    pool.tensor_tensor(splace[:, :], pick[:, m4.par, 2:4], sign2, ALU.mult).then_inc(s["sp1"], 1)
                    pool.wait_ge(s["sb1"], m4.n + 1)
                    pool.tensor_tensor(sbase[:, :], sbase[:, :], off2, ALU.add).then_inc(s["sb2"], 1)
                    pool.wait_ge(s["sp1"], m4.n + 1)
                    pool.wait_ge(s["over_done"], m4.n + 1)
                    pool.tensor_tensor(splace[:, :], splace[:, :], over[:, :], ALU.add).then_inc(s["sb3"], 1)
                    pool.wait_ge(s["sb2"], m4.n + 1)
                    pool.wait_ge(s["sb3"], m4.n + 1)
                    pool.tensor_tensor(slot_f[:, :], sbase[:, :], splace[:, :], ALU.add).then_inc(s["slot_sum"], 1)
                    need(pool, ids_sent[(m4.c + 2) % NC], (m4.b + m4.c // 2) * 32)
                    hold(pool, s["slot_sum"], m4.n + 1, s["pool_held"])
                    pool.tensor_copy(slot[:, m4.par, :], slot_f[:, :]).then_inc(s["slot_done"], 1)
                    hold(pool, ids_sent[m4.c], m4.b * 32, s["pool_held"])
                    pool.tensor_scalar(token[:, m4.c, :], token[:, m4.c, :], float(T), None, ALU.add)\
                        .then_inc(s["token_set"], 1)
                    hold(pool, s["token_set"], m4.n + 1, s["pool_held"])
                    hold(pool, s["slot_done"], m4.n + 1, s["pool_held"])
                    for j in range(TOPK):
                        pool.indirect_dma_start(slot_ids, bass.IndirectOffsetOnAxis(ap=slot[:, m4.par, j:j + 1], axis=0),
                                                token[:, m4.c, j:j + 1], None, bounds_check=TOPK * SLOTS - 1,
                                                oob_is_err=False).then_inc(ids_sent[m4.c], 16)

            steps(pool, step)
            for k in range(NC):
                pool.wait_ge(ids_sent[k], 32 * B)
            pool.wait_ge(s["y_zeroed"], 16 * (TOPK * N * D // P // 1024))


def phase_two(nc, top, sem, sb_, v):
    w1T, b1, w2, b2, out = (v[k] for k in ("w1T", "b1", "w2", "b2", "out"))
    x1_rows, slot_ids, y_rows = (v[k] for k in ("x1_rows", "slot_ids", "y_rows"))
    x1_all, top_all, pick_all, count = (v[k] for k in ("x1_all", "top_all", "pick_all", "count"))
    ident, iota8, slot_no = (v[k] for k in ("ident", "iota8", "slot_no"))
    UE = UNITS // E
    PAIR = 2 * UE
    GROUP = 4

    with ExitStack() as ctx:
        def sb(name, shape, dt=F32):
            return ctx.enter_context(nc.sbuf_tensor(name, shape, dt))

        def psum(name, shape):
            return ctx.enter_context(nc.psum_tensor(name, shape, F32))

        w1_raw = sb("w1_raw", [P, KD, H])
        w2_raw = sb("w2_raw", [P, HB, D])
        w1_hi, w1_lo = (sb(f"w1_{x}", [P, 2, KD, H], F32R) for x in ("hi", "lo"))
        w2_hi, w2_lo = (sb(f"w2_{x}", [P, 2, HB, D], F32R) for x in ("hi", "lo"))
        b1_all = sb("b1_all", [P, E, HB])
        b2_all = sb("b2_all", [P, E, D])
        rows_in = sb("rows_in", [P, 2, UM, D])
        xg_hi, xg_lo = (sb(f"xg_{x}", [P, 2, KD, UT], F32R) for x in ("hi", "lo"))
        hidden = sb("hidden", [P, 2, UT])
        h_hi, h_lo = (sb(f"h_{x}", [P, 4, UT], F32R) for x in ("hi", "lo"))
        rows_out = sb("rows_out", [P, 2, UM, D])
        ids = sb("ids", [P, P])
        ids_t = sb("ids_t", [P, TOPK, SLOTS // P])
        firsts = sb("firsts", [P, SLOTS // P])
        diff = sb("diff", [P, SLOTS // P])
        dest = sb("dest", [P, SLOTS // P], I32)
        source = sb("source", [P, SLOTS // P], I32)
        dest_u = sb("dest_u", [P, 2, UM], I32)
        source_u = sb("source_u", [P, 2, UM], I32)
        share = sb("share", [P, TOPK, TILES])
        lead = sb("lead", [P, TILES])
        spread = sb("spread", [P, TILES])
        second = sb("second", [P, TILES, E])
        second_n = sb("second_n", [P, TILES, E])
        filled = sb("filled", [P, TILES])
        valid = sb("valid", [P, TOPK, TILES])
        ys = sb("ys", [P, 2, TOPK, GROUP, D])
        fin = sb("fin", [P, 2, GROUP, D])
        fstat = sb("fstat", [P, 2, GROUP, 6])
        fmean = sb("fmean", [P, 2, GROUP, 2])
        fvar = sb("fvar", [P, 2, GROUP])
        frstd = sb("frstd", [P, 2, GROUP])
        minus_half = sb("minus_half", [P, GROUP])

        ps_h = [psum(f"ps_h{i}", [P, UT]) for i in range(2)]
        ps_x = psum("ps_x", [P, KD * UT])
        ps_out = [psum(f"ps_out{i}", [P, UM * D]) for i in range(2)]

        names = """w_in bias_in ids_in ids_turned ids_out firsts_set diff_set diff_cut ids_merged dest_set source_set
        turned xhi xlo fc1_done relu_done hhi_done hlo_done fc2_done whi_done wlo_done
        picked_in picked_out act_held dve_held2 pool_held2
        spread_set lead_set share_set second_set second_cut filled_set filled_sum valid_set share_done
        ys_first ys_sum fstat_done fmean_done half_set fvar_done frstd_done fin_done""".split()
        s = {k: sem(k + "_2") for k in names}
        rows_done = [sem(f"rows_done{i}") for i in range(2)]
        gathered = [sem(f"gathered{i}") for i in range(2)]
        scattered = [sem(f"scattered{i}") for i in range(2)]
        ys_in = [sem(f"ys_in{i}") for i in range(2)]
        stored = [sem(f"stored{i}") for i in range(2)]

        block = ctx.enter_context(nc.Block())

        def pairs(eng, unit):
            with eng.Fori(0, E // 2 - 1) as i:
                for q in range(PAIR):
                    unit(i, q, False)
            for q in range(PAIR):
                unit(E // 2 - 1, q, True)

        @block.sync
        def _(sp):
            sp.dma_start(ids[:, :], slot_ids.rearrange("(c p) o -> c (p o)", p=P)).then_inc(s["ids_in"], 16)
            sp.dma_start(w1_raw[:, :, :], w1T[0]).then_inc(s["w_in"], 16)
            sp.dma_start(w2_raw[:, :, :], w2[0]).then_inc(s["w_in"], 16)
            sp.dma_start(b1_all[:, :, :], b1).then_inc(s["bias_in"], 16)
            sp.dma_start(b2_all[:, :, :], bass.AP(b2.tensor, 0, [[0, P], [D, E], [1, D]])).then_inc(s["bias_in"], 16)
            with sp.Fori(1, E) as e:
                sp.wait_ge(s["wlo_done"], e * HB)
                for raw, w in ((w1_raw, w1T), (w2_raw, w2)):
                    sp.dma_start(raw[:, :, :], w[bass.ds(e, 1)].rearrange("e p k n -> p (e k) n"))\
                      .then_inc(s["w_in"], 16)
            for i in range(2):
                sp.wait_ge(scattered[i], 16 * UM * UNITS // 2)

            def load(i, k):
                g = i * 2 + k
                need(sp, s["ys_sum"], GROUP * (g - 2) + GROUP)
                for j in range(TOPK):
                    src = y_rows[bass.ds(g * (GROUP * P) + j * N, GROUP * P), :].rearrange("(a p) d -> p a d", p=P)
                    sp.dma_start(ys[:, k, j], src).then_inc(ys_in[k], 16)

            def store(i, k):
                g = i * 2 + k
                sp.wait_ge(s["fin_done"], GROUP * (g + 1))
                sp.dma_start(out[bass.ds(g * (GROUP * P), GROUP * P), :].rearrange("(a p) d -> p a d", p=P), fin[:, k])\
                  .then_inc(stored[k], 16)

            load(0, 0)
            load(0, 1)
            with sp.Fori(0, TILES // GROUP // 2 - 1) as i:
                for k in range(2):
                    store(i, k)
                    load(i + 1, k)
            for k in range(2):
                store(TILES // GROUP // 2 - 1, k)
            for k in range(2):
                sp.wait_ge(stored[k], 16 * (TILES // GROUP // 2))

        @block.scalar
        def _(act):
            def weights(e, par, piece):
                act.wait_ge(s["w_in"], 32 * (e + 1))
                need(act, s["fc2_done"], (e - 1) * HB * UE)
                c = slice(P * piece, P * piece + P)
                act.activation(w1_hi[:, par, :, c], w1_raw[:, :, c], ACT.Copy)
                act.activation(w2_hi[:, par, piece, :], w2_raw[:, piece, :], ACT.Copy).then_inc(s["whi_done"], 1)

            def turned(u, par):
                act.wait_ge(s["turned"], u + 1)
                need(act, s["fc1_done"], (u - 1) * HB)
                for k in range(KD):
                    o = act.activation(xg_hi[:, par, k, :], ps_x[:, UT * k:UT * k + UT], ACT.Copy)
                o.then_inc(s["xhi"], 1)

            def relu(e, u, k):
                g = u * HB + k
                need(act, s["hlo_done"], g - 1)
                hold(act, s["fc1_done"], g + 1, s["act_held"])
                act.activation(hidden[:, k % 2, :], ps_h[k % 2][:, :], ACT.Relu,
                               bias=b1_all[:, bass.ds(e, 1), k:k + 1].rearrange("p a b -> p (a b)"))\
                   .then_inc(s["relu_done"], 1)

            for piece in range(HB):
                weights(0, 0, piece)
            turned(0, 0)
            act.wait_ge(s["spread_set"], 1)
            act.activation(lead[:, :], spread[:, :], ACT.Tanh, scale=0.5).then_inc(s["lead_set"], 1)
            act.wait_ge(s["bias_in"], 32)
            for k in range(2):
                relu(0, 0, k)

            def unit(i, q, last):
                u, e = i * PAIR + q, i * 2 + q // UE
                for k in range(2, HB + 2):
                    if k < HB:
                        relu(e, u, k)
                    elif not (last and q == PAIR - 1):
                        relu(i * 2 + (q + 1) // UE, u + 1, k - HB)
                    if k == 6 and not (last and q == PAIR - 1):
                        turned(u + 1, (q + 1) % 2)
                    if q % UE == 0 and not (last and q == UE):
                        weights(e + 1, (q // UE + 1) % 2, k - 2)

            pairs(act, unit)

        @block.tensor
        def _(pe):
            def three(out_, a_hi, a_lo, b_hi, b_lo, last, first):
                pe.matmul(out_, a_hi, b_hi, start=first, stop=False, skip_group_check=True)
                pe.matmul(out_, a_hi, b_lo, start=False, stop=False, skip_group_check=True)
                return pe.matmul(out_, a_lo, b_hi, start=False, stop=last, skip_group_check=True)

            def turn(u, par, nth):
                pe.wait_ge(gathered[par], 16 * UM * nth)
                need(pe, s["xlo"], u)
                for m in range(UM):
                    for k in range(KD):
                        o = pe.transpose(ps_x[:, UT * k + P * m:UT * k + P * m + P], rows_in[:, par, m, P * k:P * k + P],
                                         ident)
                o.then_inc(s["turned"], 1)

            def fc1(e, u, par, ue, k):
                g = u * HB + k
                if k == 0:
                    pe.wait_ge(s["xlo"], u + 1)
                    if ue == 0:
                        pe.wait_ge(s["wlo_done"], (e + 1) * HB)
                need(pe, s["relu_done"], g - 1)
                c = slice(P * k, P * k + P)
                for d in range(KD):
                    o = three(ps_h[k % 2][:, :], w1_hi[:, par, d, c], w1_lo[:, par, d, c],
                              xg_hi[:, ue, d, :], xg_lo[:, ue, d, :], d == KD - 1, d == 0)
                o.then_inc(s["fc1_done"], 1)

            def fc2(e, u, par, ue, k, before):
                g = u * HB + k
                pe.wait_ge(s["hlo_done"], g + 1)
                if k == 0:
                    need(pe, rows_done[ue], before)
                for m in range(UM):
                    c = slice(P * m, P * m + P)
                    o = three(ps_out[ue][:, D * m:D * m + D], h_hi[:, k % 4, c], h_lo[:, k % 4, c],
                              w2_hi[:, par, k, :], w2_lo[:, par, k, :], k == HB - 1, k == 0 and m % 2 == 0)
                o.then_inc(s["fc2_done"], 1)

            pe.wait_ge(s["ids_in"], 16)
            pe.transpose(ps_h[0][:, 0:P], ids[:, :], ident).then_inc(s["ids_turned"], 1)
            turn(0, 0, 1)
            pe.wait_ge(s["ids_out"], 1)
            for k in range(2):
                fc1(0, 0, 0, 0, k)

            def unit(i, q, last):
                u = i * PAIR + q
                for k in range(2, HB + 2):
                    if k < HB:
                        fc1(i * 2 + q // UE, u, q // UE, q % 2, k)
                    elif not (last and q == PAIR - 1):
                        fc1(i * 2 + (q + 1) // UE, u + 1, (q + 1) // UE % 2, (q + 1) % 2, k - HB)
                    fc2(i * 2 + q // UE, u, q // UE, q % 2, k - 2, i * (PAIR // 2) + q // 2)
                    if k == 6 and not (last and q == PAIR - 1):
                        turn(u + 1, (q + 1) % 2, i * (PAIR // 2) + (q + 1) // 2 + 1)

            pairs(pe, unit)

        @block.vector
        def _(dve):
            def weights(e, par, piece):
                dve.wait_ge(s["whi_done"], e * HB + piece + 1)
                c = slice(P * piece, P * piece + P)
                dve.tensor_tensor(w1_lo[:, par, :, c], w1_raw[:, :, c], w1_hi[:, par, :, c].bitcast(F32), ALU.subtract)
                dve.tensor_tensor(w2_lo[:, par, piece, :], w2_raw[:, piece, :], w2_hi[:, par, piece, :].bitcast(F32),
                                  ALU.subtract).then_inc(s["wlo_done"], 1)

            def turned(u, par):
                dve.wait_ge(s["xhi"], u + 1)
                dve.tensor_tensor(xg_lo[:, par].rearrange("p k t -> p (k t)"), ps_x[:, :],
                                  xg_hi[:, par].bitcast(F32).rearrange("p k t -> p (k t)"), ALU.subtract)\
                   .then_inc(s["xlo"], 1)

            def split(u, k):
                g = u * HB + k
                dve.wait_ge(s["relu_done"], g + 1)
                need(dve, s["fc2_done"], g - 2)
                dve.tensor_copy(h_hi[:, k % 4, :], hidden[:, k % 2, :]).then_inc(s["hhi_done"], 1)
                dve.wait_ge(s["hhi_done"], g + 1)
                dve.tensor_tensor(h_lo[:, k % 4, :], hidden[:, k % 2, :], h_hi[:, k % 4, :].bitcast(F32), ALU.subtract)\
                   .then_inc(s["hlo_done"], 1)

            dve.tensor_tensor(firsts[:, :].rearrange("p (e k) -> p e k", e=E), slot_no,
                              count[:, 0:E].unsqueeze(2).to_broadcast([P, E, CAP // P]), ALU.is_lt)\
               .then_inc(s["firsts_set"], 1)
            dve.wait_ge(s["ids_turned"], 1)
            dve.tensor_copy(ids_t[:, :, :].rearrange("p j c -> p (j c)"), ps_h[0][:, 0:P]).then_inc(s["ids_out"], 1)
            dve.wait_ge(s["ids_out"], 1)
            dve.tensor_tensor(diff[:, :], ids_t[:, 0, :], ids_t[:, 1, :], ALU.subtract).then_inc(s["diff_set"], 1)
            dve.wait_ge(s["diff_set"], 1)
            dve.wait_ge(s["firsts_set"], 1)
            dve.tensor_tensor(diff[:, :], diff[:, :], firsts[:, :], ALU.mult).then_inc(s["diff_cut"], 1)
            dve.wait_ge(s["diff_cut"], 1)
            dve.tensor_tensor(dest[:, :], diff[:, :], ids_t[:, 1, :], ALU.add).then_inc(s["dest_set"], 1)
            dve.wait_ge(s["dest_set"], 1)
            dve.tensor_scalar(source[:, :], dest[:, :], N - 1, None, ALU.bitwise_and).then_inc(s["source_set"], 1)
            dve.tensor_tensor(spread[:, :], top_all[:, :, 0], top_all[:, :, 1], ALU.subtract)\
               .then_inc(s["spread_set"], 1)
            for piece in range(HB):
                weights(0, 0, piece)
            turned(0, 0)
            for k in range(2):
                split(0, k)
            dve.tensor_tensor(second[:, :, :], iota8[:, 0:1, :].to_broadcast([P, TILES, E]),
                              pick_all[:, :, 1:2].to_broadcast([P, TILES, E]), ALU.is_equal).then_inc(s["second_set"], 1)
            dve.wait_ge(s["second_set"], 1)
            dve.tensor_tensor(second_n[:, :, :], second[:, :, :],
                              count[:, 0:E].unsqueeze(1).to_broadcast([P, TILES, E]), ALU.mult)\
               .then_inc(s["second_cut"], 1)
            dve.wait_ge(s["second_cut"], 1)
            dve.tensor_reduce(filled[:, :], second_n[:, :, :], AX, ALU.add).then_inc(s["filled_set"], 1)
            dve.wait_ge(s["filled_set"], 1)
            dve.tensor_tensor(filled[:, :], filled[:, :], pick_all[:, :, 3], ALU.add).then_inc(s["filled_sum"], 1)
            dve.tensor_scalar(valid[:, 0, :], pick_all[:, :, 2], float(CAP), None, ALU.is_lt).then_inc(s["valid_set"], 1)
            dve.wait_ge(s["filled_sum"], 1)
            dve.tensor_scalar(valid[:, 1, :], filled[:, :], float(CAP), None, ALU.is_lt).then_inc(s["valid_set"], 1)
            dve.wait_ge(s["lead_set"], 1)
            for j in range(TOPK):
                dve.tensor_scalar(share[:, j, :], lead[:, :], 0.5 - j, 0.5, ALU.mult, ALU.add).then_inc(s["share_set"], 1)
            dve.wait_ge(s["share_set"], 2)
            dve.wait_ge(s["valid_set"], 2)
            dve.tensor_tensor(share[:, :, :], share[:, :, :], valid[:, :, :], ALU.mult).then_inc(s["share_done"], 1)
            dve.wait_ge(s["bias_in"], 32)

            def unit(i, q, last):
                u = i * PAIR + q
                for k in range(2, HB + 2):
                    if k < HB:
                        split(u, k)
                    elif not (last and q == PAIR - 1):
                        split(u + 1, k - HB)
                    if k == 6 and not (last and q == PAIR - 1):
                        turned(u + 1, (q + 1) % 2)
                    if q % UE == 0 and not (last and q == UE):
                        weights(i * 2 + q // UE + 1, (q // UE + 1) % 2, k - 2)
                dve.wait_ge(s["fc2_done"], (u + 1) * HB)
                need(dve, scattered[q % 2], (i * (PAIR // 2) + q // 2) * 16 * UM)
                bias = b2_all[:, bass.ds(i * 2 + q // UE, 1), :].to_broadcast([P, 2, D])
                for m in range(0, UM, 2):
                    o = dve.tensor_tensor(rows_out[:, q % 2, m:m + 2, :],
                                          ps_out[q % 2][:, D * m:D * m + 2 * D].rearrange("p (m d) -> p m d", m=2),
                                          bias, ALU.add)
                o.then_inc(rows_done[q % 2], 1)

            pairs(dve, unit)

            def group(i, k):
                g = i * 2 + k
                dve.wait_ge(s["share_done"], 1)
                need(dve, stored[k], i * 16)
                dve.wait_ge(ys_in[k], (i + 1) * 16 * TOPK)
                tile = lambda a: g * GROUP + a
                for a in range(GROUP):
                    dve.scalar_tensor_tensor(ys[:, k, 0, a, :], ys[:, k, 0, a, :],
                                             share[:, 0, bass.ds(tile(a), 1)],
                                             x1_all[:, bass.ds(tile(a), 1), :].rearrange("p a d -> p (a d)"),
                                             ALU.mult, ALU.add).then_inc(s["ys_first"], 1)
                for a in range(GROUP):
                    dve.wait_ge(s["ys_first"], tile(a) + 1)
                    dve.scalar_tensor_tensor(fin[:, k, a, :], ys[:, k, 1, a, :],
                                             share[:, 1, bass.ds(tile(a), 1)], ys[:, k, 0, a, :],
                                             ALU.mult, ALU.add).then_inc(s["ys_sum"], 1)
                for a in range(GROUP):
                    dve.wait_ge(s["ys_sum"], tile(a) + 1)
                    dve.bn_stats(fstat[:, k, a, :], fin[:, k, a, :]).then_inc(s["fstat_done"], 1)
                for a in range(GROUP):
                    hold(dve, s["fstat_done"], tile(a) + 1, s["dve_held2"])
                    dve.bn_aggr(fmean[:, k, a, :], fstat[:, k, a, :]).then_inc(s["fmean_done"], 1)

            def finish(i, k):
                g = i * 2 + k
                dve.wait_ge(s["frstd_done"], g + 1)
                for a in range(GROUP):
                    dve.tensor_scalar(fin[:, k, a, :], fin[:, k, a, :], fmean[:, k, a, 0:1], frstd[:, k, a:a + 1],
                                      ALU.subtract, ALU.mult).then_inc(s["fin_done"], 1)

            group(0, 0)
            with dve.Fori(0, TILES // GROUP // 2 - 1) as i:
                group(i, 1)
                finish(i, 0)
                group(i + 1, 0)
                finish(i, 1)
            last = TILES // GROUP // 2 - 1
            group(last, 1)
            finish(last, 0)
            finish(last, 1)

        @block.gpsimd
        def _(pool):
            def gather(u, par):
                hold(pool, s["turned"], u - 1, s["pool_held2"])
                pool.tensor_copy(source_u[:, par, :], source[:, bass.ds(u * UM, UM)]).then_inc(s["picked_in"], 1)
                hold(pool, s["picked_in"], u + 1, s["pool_held2"])
                for m in range(UM):
                    pool.indirect_dma_start(rows_in[:, par, m, :], None, x1_rows,
                                            bass.IndirectOffsetOnAxis(ap=source_u[:, par, m:m + 1], axis=0))\
                        .then_inc(gathered[par], 16)

            def scatter(u, par, nth):
                hold(pool, scattered[par], nth * 16 * UM, s["pool_held2"])
                pool.tensor_copy(dest_u[:, par, :], dest[:, bass.ds(u * UM, UM)]).then_inc(s["picked_out"], 1)
                hold(pool, s["picked_out"], u + 1, s["pool_held2"])
                hold(pool, rows_done[par], nth + 1, s["pool_held2"])
                for m in range(UM):
                    pool.indirect_dma_start(y_rows, bass.IndirectOffsetOnAxis(ap=dest_u[:, par, m:m + 1], axis=0),
                                            rows_out[:, par, m, :], None, bounds_check=TOPK * N - 1, oob_is_err=False)\
                        .then_inc(scattered[par], 16)

            pool.memset(minus_half[:, :], -0.5).then_inc(s["half_set"], 1)
            pool.wait_ge(s["half_set"], 1)
            pool.wait_ge(s["source_set"], 1)
            gather(0, 0)
            gather(1, 1)

            def unit(i, q, last):
                u = i * PAIR + q
                scatter(u, q % 2, i * (PAIR // 2) + q // 2)
                if not (last and q >= PAIR - 2):
                    gather(u + 2, q % 2)

            pairs(pool, unit)

            def root(i, k):
                g = i * 2 + k
                hold(pool, s["fmean_done"], GROUP * (g + 1), s["pool_held2"])
                pool.tensor_scalar(fvar[:, k, :], fmean[:, k, :, 1], EPS, None, ALU.add).then_inc(s["fvar_done"], 1)
                pool.wait_ge(s["fvar_done"], g + 1)
                pool.tensor_tensor(frstd[:, k, :], fvar[:, k, :], minus_half[:, :], ALU.pow).then_inc(s["frstd_done"], 1)

            with pool.Fori(0, TILES // GROUP // 2) as i:
                for k in range(2):
                    root(i, k)


def _tables():
    f = np.float32
    pos = np.arange(T, dtype=f)
    freq = f(1) / (10000.0 ** (np.arange(D // 2) / (D // 2))).astype(f)
    phase = (pos[:, None] * freq[None, :]).astype(np.float64)
    width = ((np.arange(0, D, 2) + 0.4 * D) / (1.4 * D)).astype(f).astype(np.float64)
    grow = width[None, :] ** (pos[:, None].astype(np.float64) / 512.0)
    rope = np.zeros((2, T, 2, D), np.float64)
    for i, scale in enumerate((grow * DK ** -0.5, 1.0 / grow)):
        rope[0, :, i, :] = np.repeat(np.cos(phase) * scale, 2, axis=1)
        rope[1, :, i, 0::2] = -np.sin(phase) * scale
        rope[1, :, i, 1::2] = np.sin(phase) * scale
    rope = rope.reshape(2, NC, P, 2 * D).transpose(0, 2, 1, 3).astype(f)
    p = np.arange(P)
    token = [[[j * N + c * P - T for j in range(TOPK)] for c in range(NC)]]
    parts = [
        np.eye(P),
        (p[:, None] < p[None, :]),
        np.tile(np.arange(E), (P, TOPK)),
        np.tile([1, -1], (P, 1)),
        np.tile([0, SLOTS + CAP - 1], (P, 1)),
        (np.array(token) + p[:, None, None]).reshape(P, NC * TOPK),
        np.tile(np.arange(CAP // P) * P, (P, E)) + p[:, None],
    ]
    return np.ascontiguousarray(rope), np.concatenate(parts, axis=1).astype(f)


def kernel(**inputs):
    import numpy as _np
    import concourse.bacc as _bacc
    from concourse import mybir as _mybir
    from concourse.bass_utils import run_bass_kernel_spmd as _run

    x, w_qkv, w_gated, w_proj, decay, gate_w, w1, b1, w2, b2 = (
        _np.asarray(inputs[k]) for k in (
            "L0_attn_hidden_states", "L0_attn_w_qkv", "L0_attn_w_gated", "L0_attn_w_proj", "L0_attn_decay",
            "L0_ffn_gate_w", "L0_ffn_fc1_w", "L0_ffn_fc1_b", "L0_ffn_fc2_w", "L0_ffn_fc2_b"))
    rows = x.reshape(N, D)
    rope, consts = _tables()
    arrays = {
        "xT": rows.T.reshape(KD, P, N).transpose(1, 0, 2),
        "xk": rows,
        "wT": _np.concatenate([w_qkv, w_gated], axis=0).T.reshape(KD, P, -1).transpose(1, 0, 2),
        "wpT": w_proj.T.reshape(VD // P, P, D).transpose(1, 0, 2),
        "decay": decay.reshape(NH, 1),
        "gwT": gate_w.T.reshape(KD, P, E).transpose(1, 0, 2),
        "w1T": w1.transpose(0, 2, 1).reshape(E, KD, P, H).transpose(0, 2, 1, 3),
        "b1": b1.reshape(E, HB, P).transpose(2, 0, 1),
        "w2": w2.reshape(E, HB, P, D).transpose(0, 2, 1, 3),
        "b2": b2.reshape(E, D),
        "rope": rope,
        "consts": consts,
    }
    arrays = {f"in_{k}": _np.ascontiguousarray(a) for k, a in arrays.items()}
    nc = _bacc.Bacc("TRN2", target_bir_lowering=False, num_devices=1)
    args = [nc.dram_tensor(k, a.shape, _mybir.dt.from_np(a.dtype), kind="ExternalInput").ap() for k, a in arrays.items()]
    args.append(nc.dram_tensor("out_0", (N, D), F32, kind="ExternalOutput").ap())
    moe_layer(nc, *args)
    r = _run(nc, [arrays], core_ids=[0])
    return r.results[0]["out_0"].reshape(B, T, D)
```

```python
from contextlib import ExitStack

import numpy as np

import concourse.bass as bass
from concourse import mybir
from concourse.alu_op_type import AluOpType as ALU

F32 = mybir.dt.float32
F32R = mybir.dt.float32r
BF16 = mybir.dt.bfloat16
I32 = mybir.dt.int32
U32 = mybir.dt.uint32
ACT = mybir.ActivationFunctionType
AX = mybir.AxisListType.X

P = 128
B, T, D = 8, 512, 256
NH, DK, DV = 8, 32, 64
VD = NH * DV
NC = T // P
N = B * T
TILES = N // P
KD = D // P
E, H, TOPK = 8, 1024, 2
CAP = TOPK * N // E
SLOTS = E * CAP
HB = H // P
UT = 512
UM = UT // P
UNITS = SLOTS // UT
EPS = 1e-5
SKIP = 65536.0
LASTLAG = 4


def need(eng, sem, value):
    if not isinstance(value, int) or value > 0:
        eng.wait_ge(sem, value)


def hold(eng, sem, value, held):
    if not isinstance(value, int) or value > 0:
        eng.wait_ge(sem, value)
        eng.sem_inc(held, 1)


class Chunk:

    def __init__(self, b, c, lag=0):
        self.c = (c - lag) % NC
        self.b = b + (c - lag) // NC
        self.n = self.b * NC + self.c
        self.live = not isinstance(self.n, int) or 0 <= self.n < TILES
        self.par = self.c % 2

    def uses(self):
        return self.b * (NC // 2) + self.c // 2


def steps(eng, step):
    for b in range(2):
        for c in range(NC):
            step(b, c)
    with eng.Fori(2, B - 1) as b:
        for c in range(NC):
            step(b, c)
    for c in range(NC):
        step(B - 1, c)
    for c in range(LASTLAG):
        step(B, c)


def moe_layer(nc, xT, xk, wT, wpT, decay, gwT, w1T, b1, w2, b2, rope, consts, out):
    with ExitStack() as top:
        def dram(name, shape, dt=F32):
            return nc.dram_tensor(name, shape, dt, kind="Internal").ap()

        def sem(name):
            return top.enter_context(nc.semaphore(name))

        def sb(name, shape, dt=F32, ctx=top):
            return ctx.enter_context(nc.sbuf_tensor(name, shape, dt))

        decay_rows = dram("decay_rows", [NH, 512])
        x1_rows = dram("x1_rows", [N, D])
        slot_ids = dram("slot_ids", [TOPK * SLOTS, 1])
        y_rows = dram("y_rows", [TOPK * N, D])

        x1_all = sb("x1_all", [P, TILES, D])
        top_all = sb("top_all", [P, TILES, 2])
        pick_all = sb("pick_all", [P, TILES, 4])
        count = sb("count", [P, TOPK * E])
        const = sb("const", [P, consts.shape[1]])
        landing = sb("landing", [P, KD * H + HB * D])
        w1_raw = landing[:, 0:KD * H].rearrange("p (k n) -> p k n", k=KD)
        w2_raw = landing[:, KD * H:].rearrange("p (k n) -> p k n", k=HB)
        expert_in = sem("expert_in")
        ident = const[:, 0:128]
        iota8 = const[:, 256:272].rearrange("p (j e) -> p j e", e=E)
        sign2 = const[:, 272:274]
        off2 = const[:, 274:276]
        token0 = const[:, 276:284].rearrange("p (c j) -> p c j", j=2)
        slot_no = const[:, 284:348].rearrange("p (e k) -> p e k", e=E)

        phase_one(nc, sem, locals())
        phase_two(nc, sem, locals())


def phase_one(nc, sem, v):
    xT, xk, wT, wpT, decay, gwT = (v[k] for k in ("xT", "xk", "wT", "wpT", "decay", "gwT"))
    rope, consts = v["rope"], v["consts"]
    decay_rows, x1_rows, slot_ids, y_rows = (v[k] for k in ("decay_rows", "x1_rows", "slot_ids", "y_rows"))
    x1_all, top_all, pick_all, count, const = (v[k] for k in ("x1_all", "top_all", "pick_all", "count", "const"))
    ident, iota8, sign2, off2, token0 = (v[k] for k in ("ident", "iota8", "sign2", "off2", "token0"))
    before = const[:, 128:256]

    with ExitStack() as ctx:
        def sb(name, shape, dt=F32):
            return ctx.enter_context(nc.sbuf_tensor(name, shape, dt))

        def psum(name, shape):
            return ctx.enter_context(nc.psum_tensor(name, shape, F32))

        W3 = 2 * D + 2 * VD
        w_hi, w_lo = (sb(f"w_{x}", [P, KD, W3], F32R) for x in ("hi", "lo"))
        wp_hi, wp_lo = (sb(f"wp_{x}", [P, VD // P, D], F32R) for x in ("hi", "lo"))
        raw = x1_all[:, :, :].rearrange("p t d -> p (t d)")
        w_raw = raw[:, 0:KD * W3].rearrange("p (k n) -> p k n", k=KD)
        wp_raw = raw[:, KD * W3:KD * W3 + VD * 2].rearrange("p (k n) -> p k n", n=D)
        gw = sb("gw", [P, KD, 96])
        cos_t = sb("cos_t", [P, NC, 2 * D])
        sin_t = sb("sin_t", [P, NC, 2 * D])
        drow = sb("drow", [NH, 512])
        dpow = sb("dpow", [NH, 8])
        fade = sb("fade", [P, NH, P])
        fade_q = sb("fade_q", [P, 2, P])
        fade_k = fade[:, :, P - 1:P]
        fade_c = fade_q[:, :, P - 1]
        vmean = sb("vmean", [P, KD, NH])
        before_b = sb("before_b", [P, P], BF16)
        ones_b = sb("ones_b", [P, P], BF16)
        half_neg = sb("half_neg", [P, NH])
        token = sb("token", [P, NC, 2])
        zeros = sb("zeros", [P, 1024])

        xt_raw = sb("xt_raw", [P, NC, KD, P])
        xt_hi, xt_lo = (sb(f"xt_{x}", [P, NC, KD, P], F32R) for x in ("hi", "lo"))
        x_tok = sb("x_tok", [P, NC, D])
        rot_a = sb("rot_a", [P, 2 * D])
        rot_b = sb("rot_b", [P, 2 * D])
        qk = sb("qk", [P, 2, 2 * D])
        k_fade = sb("k_fade", [P, 2, D])
        k_t = sb("k_t", [P, 2, 2, P])
        q_diag = sb("q_diag", [P, 2, 2, 4, P])
        q_fade = sb("q_fade", [P, 2, 2, P])
        v_pad = sb("v_pad", [P, 2, NH, P])
        probs = sb("probs", [P, 2, NH, P])
        gate = sb("gate", [P, 2, VD])
        state = sb("state", [P, 2, 2, 4 * DV])
        square = sb("square", [P, VD])
        ssum = sb("ssum", [P, 2, NH])
        svar = sb("svar", [P, NH])
        srstd = sb("srstd", [P, 2, NH])
        normed = sb("normed", [P, VD])
        gated = sb("gated", [P, 2, VD])
        gt_hi, gt_lo = (sb(f"gt_{x}", [P, VD // P, P], F32R) for x in ("hi", "lo"))
        z = sb("z", [P, 2, D])
        zstat = sb("zstat", [P, 2, 6])
        zmean = sb("zmean", [P, 2, 2])
        zvar = sb("zvar", [P, 1])
        zrstd = sb("zrstd", [P, 2, 1])
        x1 = sb("x1", [P, 2, D])
        x1_t = sb("x1_t", [P, KD, P])
        logit = sb("logit", [P, E])
        best = sb("best", [P, 8])
        besti = sb("besti", [P, 8], U32)
        pick = sb("pick", [P, 2, 4])
        hot = sb("hot", [P, TOPK * E], BF16)
        place = sb("place", [P, TOPK * E])
        over = sb("over", [P, 2])
        sbase = sb("sbase", [P, 2])
        splace = sb("splace", [P, 2])
        slot_f = sb("slot_f", [P, 2])
        slot = sb("slot", [P, 2, 2], I32)

        ps_qk = psum("ps_qk", [P, 512])
        ps_v = psum("ps_v", [P, 512])
        ps_g = psum("ps_g", [P, 512])
        ps_t = psum("ps_t", [P, 512])
        ps_s = psum("ps_s", [P, 1024])
        ps_o = psum("ps_o", [P, 512])
        ps_y = psum("ps_y", [P, 512])

        names = """const_in decay_in drow_out fades_in fade_set gw_in ids_set y_zeroed
        centred drow_ready fixed small_set zero_set
        qk_done v_done g_done t_done s_done o_done u_done n_done y_done xt_done l_done c_done
        xhi_done v_out gate_done t_out square_done ghi_done x1t_out
        xlo_done rotated qfade_done probs_done state_done ssum_done normed_done gated_done glo_done z_done
        zstat_done zmean_done x1_done logit_out best_done besti_done pick_set hot_done place_sum place_mul
        place_done count_done
        setup_step dve_held pool_held qk_sum kfade_done svar_done srstd_done zvar_done zrstd_done slot_step
        slot_done token_set""".split()
        s = {k: sem(k) for k in names}
        w_in, w_hi_done, w_lo_done = ([sem(f"{x}{j}") for j in range(4)] for x in ("w_in", "w_hi_done", "w_lo_done"))
        rope_in = [sem(f"rope_in{c}") for c in range(NC)]
        xt_in = [sem(f"xt_in{c}") for c in range(NC)]
        xk_in = [sem(f"xk_in{c}") for c in range(NC)]
        x1_saved = [sem(f"x1_saved{c}") for c in range(2)]
        ids_sent = [sem(f"ids_sent{c}") for c in range(NC)]

        col = [slice(512 * j, 512 * j + 512) for j in range(3)]
        parts = [(w_raw[:, :, c], w_hi[:, :, c], w_lo[:, :, c]) for c in col]
        parts.append((wp_raw, wp_hi[:, :, :], wp_lo[:, :, :]))

        block = ctx.enter_context(nc.Block())

        @block.sync
        def _(sp):
            def load_columns(m):
                need(sp, s["xlo_done"], m.n - NC + 1)
                sp.dma_start(xt_raw[:, m.c], xT[:, :, bass.ds(m.n * P, P)]).then_inc(xt_in[m.c], 16)

            def load_rows(m):
                need(sp, s["z_done"], m.n - NC + 1)
                sp.dma_start(x_tok[:, m.c, :], xk[bass.ds(m.n * P, P), :]).then_inc(xk_in[m.c], 16)

            def load_rope(c):
                for t, row in ((cos_t, 0), (sin_t, 1)):
                    sp.dma_start(t[:, c, :], rope[row][:, c, :]).then_inc(rope_in[c], 16)

            sp.dma_start(dpow[:, 0:1], decay).then_inc(s["decay_in"], 16)
            load_columns(Chunk(0, 0))
            for j in (0, 1, 2):
                sp.dma_start(w_raw[:, :, col[j]], wT[:, :, col[j]]).then_inc(w_in[j], 16)
            sp.dma_start(const[:, :], consts).then_inc(s["const_in"], 16)
            sp.dma_start(gw[:, :, 0:E], gwT).then_inc(s["gw_in"], 16)
            load_rope(0)
            sp.wait_ge(s["drow_ready"], 1)
            sp.dma_start(decay_rows, drow[:, :]).then_inc(s["drow_out"], 16)
            sp.dma_start(wp_raw, wpT).then_inc(w_in[3], 16)
            load_columns(Chunk(0, 1))
            sp.wait_ge(s["drow_out"], 16)
            rows = decay_rows.tensor
            sp.dma_start(probs[:, 0], bass.AP(rows, 257, [[1, P], [512, NH], [1, P]])).then_inc(s["fades_in"], 16)
            for j in range(4):
                sp.dma_start(fade_q[DK * j:DK * j + DK, :, :],
                             bass.AP(rows, 512 * j + 128, [[0, DK], [2048, 2], [1, P]])).then_inc(s["fades_in"], 16)
            for c in range(2, NC):
                load_columns(Chunk(0, c))
            for c in range(1, NC):
                load_rope(c)
            for c in range(NC):
                load_rows(Chunk(0, c))
            sp.wait_ge(s["zero_set"], 2)
            sp.dma_start(slot_ids.rearrange("(p c) o -> p (c o)", p=P), zeros[:, 0:P]).then_inc(s["ids_set"], 16)
            sp.wait_ge(s["zero_set"], 4)
            y_zero = y_rows.rearrange("(p a) d -> p (a d)", p=P)

            def step(b, c):
                m = Chunk(b + 1, c)
                if m.live and Chunk(b, c).live:
                    load_columns(m)
                if Chunk(b, c).live and c % 2 == 0:
                    sp.dma_start(y_zero[:, bass.ds((b * 2 + c // 2) * 1024, 1024)], zeros[:, :])\
                      .then_inc(s["y_zeroed"], 16)
                m = Chunk(b, c, 2)
                if m.live:
                    if isinstance(m.n, int) and m.n == 0:
                        for j in range(4):
                            sp.wait_ge(w_lo_done[j], 1)
                    sp.wait_ge(s["x1_done"], m.n + 1)
                    sp.dma_start(x1_all[:, bass.ds(m.n, 1), :].rearrange("p a d -> p (a d)"), x1[:, m.par, :])\
                      .then_inc(x1_saved[m.par], 16)
                    sp.dma_start(x1_rows[bass.ds(m.n * P, P), :], x1[:, m.par, :]).then_inc(x1_saved[m.par], 16)
                    m = Chunk(m.b + 1, m.c)
                    if m.live:
                        load_rows(m)
                if isinstance(b, int) and b == 1 and c == 0:
                    sp.dma_start(v["w1_raw"], v["w1T"][0]).then_inc(v["expert_in"], 16)
                    sp.dma_start(v["w2_raw"], v["w2"][0]).then_inc(v["expert_in"], 16)

            steps(sp, step)
            for k in range(2):
                sp.wait_ge(x1_saved[k], 32 * TILES // 2)
            sp.wait_ge(v["expert_in"], 32)

        @block.scalar
        def _(act):
            def split_x(m):
                act.wait_ge(xt_in[m.c], (m.b + 1) * 16)
                need(act, s["g_done"], m.n - NC + 1)
                act.activation(xt_hi[:, m.c], xt_raw[:, m.c], ACT.Copy).then_inc(s["xhi_done"], 1)

            def split_weights(j):
                act.wait_ge(w_in[j], 16)
                raw, high, _ = parts[j]
                act.activation(high, raw, ACT.Copy).then_inc(w_hi_done[j], 1)

            split_x(Chunk(0, 0))
            split_weights(0)
            split_weights(2)
            act.wait_ge(s["centred"], 1)
            split_weights(1)
            split_x(Chunk(0, 1))
            act.wait_ge(s["small_set"], 4)

            def step(b, c):
                m = Chunk(b, c, 1)
                if m.live:
                    act.wait_ge(s["o_done"], m.n + 1)
                    need(act, s["ssum_done"], m.n)
                    act.activation(square[:, :], ps_o[:, :], ACT.Square).then_inc(s["square_done"], 1)
                m = Chunk(b, c)
                if m.live:
                    act.wait_ge(s["v_done"], m.n + 1)
                    need(act, s["o_done"], m.n - 1)
                    vv = v_pad[:, m.par].rearrange("p (a two) (f c) -> p a (two f) c", two=2, c=DV)
                    act.activation(vv[:, :, ::3, :], ps_v[:, :].rearrange("p (a f c) -> p a f c", f=2, c=DV), ACT.Copy)\
                       .then_inc(s["v_out"], 1)
                    act.wait_ge(s["t_done"], m.n + 1)
                    need(act, s["s_done"], m.n - 1)
                    act.activation(k_t[:, m.par], ps_t[:, 2 * P:4 * P].rearrange("p (g t) -> p g t", g=2), ACT.Copy)
                    for j in range(4):
                        r = slice(DK * j, DK * j + DK)
                        o = act.activation(q_diag[r, m.par, :, j, :],
                                           ps_t[r, 0:2 * P].rearrange("p (g t) -> p g t", g=2), ACT.Copy)
                    o.then_inc(s["t_out"], 1)
                    act.wait_ge(s["g_done"], m.n + 1)
                    need(act, s["gated_done"], m.n - 1)
                    act.activation(gate[:, m.par, :], ps_g[:, :], ACT.Silu).then_inc(s["gate_done"], 1)
                    if isinstance(m.n, int) and m.n == 0:
                        split_x(Chunk(0, 2))
                        split_x(Chunk(0, 3))
                        split_weights(3)
                m = Chunk(b, c, 1)
                if m.live:
                    act.wait_ge(s["n_done"], m.n + 1)
                    need(act, s["y_done"], m.n)
                    act.activation(gt_hi[:, :, :].rearrange("p k t -> p (k t)"), ps_t[:, :], ACT.Copy)\
                       .then_inc(s["ghi_done"], 1)
                m = Chunk(b, c, 3)
                if m.live:
                    act.wait_ge(s["xt_done"], m.n + 1)
                    need(act, s["l_done"], m.n)
                    act.activation(x1_t[:, :, :].rearrange("p k t -> p (k t)"), ps_y[:, 0:D], ACT.Copy)\
                       .then_inc(s["x1t_out"], 1)
                m = Chunk(b + 1, c)
                if m.live and Chunk(b, c).live:
                    split_x(m)

            steps(act, step)

        @block.tensor
        def _(pe):

            def weights_ready(m, j):
                if isinstance(m.n, int) and m.n == 0:
                    pe.wait_ge(w_hi_done[j], 1)
                    pe.wait_ge(w_lo_done[j], 1)

            def three(out_, a_hi, a_lo, b_hi, b_lo, last, first=True):
                pe.matmul(out_, a_hi, b_hi, start=first, stop=False)
                pe.matmul(out_, a_hi, b_lo, start=False, stop=False)
                return pe.matmul(out_, a_lo, b_hi, start=False, stop=last)

            def project(out_, m, col):
                for k in range(KD):
                    o = three(out_, xt_hi[:, m.c, k, :], xt_lo[:, m.c, k, :], w_hi[:, k, col:col + 512],
                              w_lo[:, k, col:col + 512], k == KD - 1, k == 0)
                return o

            def step(b, c):
                m0, m1, m2, m3, m4 = (Chunk(b, c, lag) for lag in range(5))
                if m0.live:
                    pe.wait_ge(s["xlo_done"], m0.n + 1)
                    need(pe, s["rotated"], 2 * m0.n)
                    weights_ready(m0, 0)
                    project(ps_qk[:, :], m0, 0).then_inc(s["qk_done"], 1)
                if m4.live:
                    pe.wait_ge(s["x1t_out"], m4.n + 1)
                    for k in range(KD):
                        o = pe.matmul(ps_y[:, 256:352], x1_t[:, k, :], gw[:, k, :], start=k == 0, stop=k == KD - 1)
                    o.then_inc(s["l_done"], 1)
                if m1.live:
                    need(pe, s["normed_done"], m1.n)
                    pe.wait_ge(s["probs_done"], m1.n + 1)
                    pe.wait_ge(s["v_out"], m1.n + 1)
                    if m1.c > 0:
                        pe.wait_ge(s["qfade_done"], m1.n + 1)
                        pe.wait_ge(s["state_done"], m1.b * (NC - 1) + m1.c)
                        for g in range(2):
                            pe.matmul(ps_o[:, 256 * g:256 * g + 256], q_fade[:, m1.par, g, :], state[:, m1.par, g, :],
                                      start=g == 0, stop=False, skip_group_check=True)
                    for h in range(NH):
                        pair = h // 2
                        o = pe.matmul(ps_o[:, P * pair:P * pair + P], probs[:, m1.par, h, :], v_pad[:, m1.par, h, :],
                                      start=(m1.c == 0 and h == 0), stop=(h == NH - 1), skip_group_check=True)
                    o.then_inc(s["o_done"], 1)
                if m0.live:
                    full = m0.b * (NC - 1) + min(m0.c, NC - 1)
                    need(pe, s["state_done"], full)
                    need(pe, s["v_out"], m0.n)
                    weights_ready(m0, 1)
                    if isinstance(m0.n, int) and m0.n == 0:
                        for k in ("const_in", "gw_in"):
                            pe.wait_ge(s[k], 16)
                        pe.wait_ge(s["small_set"], 4)
                        pe.wait_ge(s["fixed"], 1)
                    project(ps_v[:, :], m0, 2 * D).then_inc(s["v_done"], 1)
                    pe.wait_ge(s["qk_sum"], m0.n + 1)
                    need(pe, s["glo_done"], m0.n - 1)
                    need(pe, s["qfade_done"], m0.n)
                    for i in range(4):
                        o = pe.transpose(ps_t[:, P * i:P * i + P], qk[:, m0.par, P * i:P * i + P], ident)
                    o.then_inc(s["t_done"], 1)
                    need(pe, s["gate_done"], m0.n)
                    weights_ready(m0, 2)
                    project(ps_g[:, :], m0, 2 * D + VD).then_inc(s["g_done"], 1)
                if m2.live:
                    pe.wait_ge(s["glo_done"], m2.n + 1)
                    need(pe, s["logit_out"], m2.n - 1)
                    need(pe, s["x1t_out"], m2.n - 1)
                    weights_ready(m2, 3)
                    for k in range(VD // P):
                        o = three(ps_y[:, 0:D], gt_hi[:, k, :], gt_lo[:, k, :], wp_hi[:, k, :], wp_lo[:, k, :],
                                  k == VD // P - 1, k == 0)
                    o.then_inc(s["y_done"], 1)
                if m0.live:
                    pe.wait_ge(s["t_out"], m0.n + 1)
                    need(pe, s["probs_done"], m0.n)
                    for g in range(2):
                        o = pe.matmul(ps_s[:, 512 * g:512 * g + 512], k_t[:, m0.par, g, :],
                                      q_diag[:, m0.par, g].rearrange("p j t -> p (j t)"), start=True, stop=True)
                    o.then_inc(s["s_done"], 1)
                if m4.live:
                    pe.wait_ge(s["hot_done"], m4.n + 1)
                    if m2.live:
                        pe.wait_ge(s["z_done"], m2.n + 1)
                    pe.matmul(ps_y[:, 384:400], before_b[:, :], hot[:, :], start=True, stop=True)
                    pe.matmul(ps_y[:, 400:416], ones_b[:, :], hot[:, :], start=True, stop=True)\
                      .then_inc(s["c_done"], 1)
                if m0.live and m0.c < NC - 1:
                    pe.wait_ge(s["kfade_done"], m0.b * (NC - 1) + m0.c + 1)
                    pe.wait_ge(s["v_out"], m0.n + 1)
                    for g in range(2):
                        vg = v_pad[:, m0.par].rearrange("p (a two) (f c) -> p a (two f) c", two=2, c=DV)
                        vg = vg[:, 2 * g:2 * g + 2, ::3, :]
                        o = pe.matmul(ps_v[:, 256 * g:256 * g + 256], k_fade[:, m0.par, P * g:P * g + P],
                                      vg, start=True, stop=True)
                    o.then_inc(s["u_done"], 1)
                if m1.live:
                    pe.wait_ge(s["gated_done"], m1.n + 1)
                    if m0.live:
                        pe.wait_ge(s["qfade_done"], m0.n + 1)
                    for i in range(4):
                        o = pe.transpose(ps_t[:, P * i:P * i + P], gated[:, m1.par, P * i:P * i + P], ident)
                    o.then_inc(s["n_done"], 1)
                if m3.live:
                    pe.wait_ge(s["x1_done"], m3.n + 1)
                    need(pe, s["count_done"], m3.n)
                    if m2.live:
                        pe.wait_ge(s["z_done"], m2.n + 1)
                    for k in range(KD):
                        o = pe.transpose(ps_y[:, P * k:P * k + P], x1[:, m3.par, P * k:P * k + P], ident)
                    o.then_inc(s["xt_done"], 1)

            steps(pe, step)

        @block.vector
        def _(dve):
            def split_x(m):
                dve.wait_ge(s["xhi_done"], m.n + 1)
                dve.tensor_tensor(xt_lo[:, m.c], xt_raw[:, m.c], xt_hi[:, m.c].bitcast(F32), ALU.subtract)\
                   .then_inc(s["xlo_done"], 1)

            passed = [0]

            def chain(instruction):
                instruction.then_inc(s["setup_step"], 1)
                passed[0] += 1
                dve.wait_ge(s["setup_step"], passed[0])

            chain(dve.memset(drow[:, :], 0.0))
            chain(dve.memset(drow[:, 127:128], 1.0))
            dve.wait_ge(s["decay_in"], 16)
            for i in range(7):
                chain(dve.tensor_tensor(dpow[:, i + 1:i + 2], dpow[:, i:i + 1], dpow[:, i:i + 1], ALU.mult))
            for i in range(7):
                w = 1 << i
                chain(dve.tensor_scalar(drow[:, 127 + w:127 + 2 * w], drow[:, 127:127 + w], dpow[:, i:i + 1],
                                             None, ALU.mult))
            chain(dve.tensor_copy(drow[:, 255:256], dpow[:, 7:8]))
            dve.tensor_copy(drow[:, 256:512], drow[:, 0:256][:, ::-1]).then_inc(s["drow_ready"], 1)
            dve.memset(gw[:, :, E:96], 0.0).then_inc(s["small_set"], 1)
            dve.memset(ones_b[:, :], 1.0)
            dve.memset(count[:, :], 0.0)
            def split_weights(j):
                raw, high, low = parts[j]
                dve.wait_ge(w_hi_done[j], 1)
                dve.tensor_tensor(low, raw, high.bitcast(F32), ALU.subtract).then_inc(w_lo_done[j], 1)

            split_x(Chunk(0, 0))
            split_weights(0)
            dve.wait_ge(w_in[1], 16)
            wv = [w_raw[:, k, 2 * D:2 * D + VD].rearrange("p (h c) -> p h c", h=NH) for k in range(KD)]
            for k in range(KD):
                chain(dve.tensor_reduce(vmean[:, k, :], wv[k], AX, ALU.add))
            chain(dve.tensor_scalar(vmean[:, :, :], vmean[:, :, :], 1.0 / DV, None, ALU.mult))
            for k in range(KD):
                o = dve.tensor_tensor(wv[k], wv[k], vmean[:, k, :].unsqueeze(2).to_broadcast([P, NH, DV]), ALU.subtract)
            o.then_inc(s["centred"], 1)
            dve.wait_ge(s["const_in"], 16)
            dve.tensor_copy(before_b[:, :], before).then_inc(s["fixed"], 1)
            dve.wait_ge(s["centred"], 1)
            split_weights(1)
            dve.wait_ge(s["small_set"], 4)

            def step(b, c):
                m0, m1, m2, m3, m4 = (Chunk(b, c, lag) for lag in range(5))
                if m0.live:
                    dve.wait_ge(s["qk_done"], m0.n + 1)
                    need(dve, s["qk_sum"], m0.n)
                    if isinstance(b, int) and b == 0:
                        dve.wait_ge(rope_in[m0.c], 32)
                    dve.tensor_tensor(rot_a[:, :], ps_qk[:, :], cos_t[:, m0.c, :], ALU.mult).then_inc(s["rotated"], 1)
                    pairs = [t.rearrange("p (f two) -> p f two", two=2)
                             for t in (rot_b[:, :], ps_qk[:, :], sin_t[:, m0.c, :])]
                    dve.tensor_tensor(pairs[0], pairs[1][:, :, ::-1], pairs[2], ALU.mult).then_inc(s["rotated"], 1)
                if m2.live:
                    dve.wait_ge(s["ghi_done"], m2.n + 1)
                    dve.tensor_tensor(gt_lo[:, :, :].rearrange("p k t -> p (k t)"), ps_t[:, :],
                                      gt_hi[:, :, :].bitcast(F32).rearrange("p k t -> p (k t)"), ALU.subtract)\
                       .then_inc(s["glo_done"], 1)
                if m3.live:
                    dve.wait_ge(s["zrstd_done"], m3.n + 1)
                    need(dve, x1_saved[m3.par], m3.uses() * 32)
                    need(dve, s["xt_done"], m3.n - 1)
                    dve.tensor_scalar(x1[:, m3.par, :], z[:, m3.par, :], zmean[:, m3.par, 0:1], zrstd[:, m3.par, :],
                                      ALU.subtract, ALU.mult).then_inc(s["x1_done"], 1)
                if m4.live:
                    dve.wait_ge(s["l_done"], m4.n + 1)
                    dve.tensor_copy(logit[:, :], ps_y[:, 256:256 + E]).then_inc(s["logit_out"], 1)
                    hold(dve, s["logit_out"], m4.n + 1, s["dve_held"])
                    dve.max(best[:, :], logit[:, :]).then_inc(s["best_done"], 1)
                    hold(dve, s["best_done"], m4.n + 1, s["dve_held"])
                    dve.max_index(besti[:, :], best[:, :], logit[:, :]).then_inc(s["besti_done"], 1)
                    dve.tensor_copy(top_all[:, bass.ds(m4.n, 1), :].rearrange("p a j -> p (a j)"), best[:, 0:2])
                    dve.wait_ge(s["besti_done"], m4.n + 1)
                    need(dve, s["slot_done"], m4.n - 1)
                    dve.tensor_copy(pick[:, m4.par, 0:2], besti[:, 0:2]).then_inc(s["pick_set"], 1)
                    dve.wait_ge(s["pick_set"], m4.n + 1)
                    need(dve, s["c_done"], m4.n)
                    dve.tensor_tensor(hot[:, :].rearrange("p (j e) -> p j e", e=E), iota8,
                                      pick[:, m4.par, 0:2].unsqueeze(2).to_broadcast([P, 2, E]), ALU.is_equal)\
                       .then_inc(s["hot_done"], 1)
                if isinstance(m0.n, int) and m0.n == 0:
                    split_x(Chunk(0, 1))
                if isinstance(m0.n, int) and m0.n == 1:
                    split_x(Chunk(0, 2))
                    split_x(Chunk(0, 3))
                if m1.live:
                    dve.wait_ge(s["square_done"], m1.n + 1)
                    need(dve, s["svar_done"], m1.n - 1)
                    dve.tensor_reduce(ssum[:, m1.par, :], square[:, :].rearrange("p (h c) -> p h c", h=NH), AX,
                                      ALU.add).then_inc(s["ssum_done"], 1)
                if m0.live:
                    dve.wait_ge(s["t_out"], m0.n + 1)
                    need(dve, s["o_done"], m0.n - 1)
                    if isinstance(m0.n, int) and m0.n == 0:
                        dve.wait_ge(s["fades_in"], 16 * 5)
                        dve.tensor_copy(fade[:, :, :], probs[:, 0, :, ::-1]).then_inc(s["fade_set"], 1)
                        dve.wait_ge(s["fade_set"], 1)
                    dve.tensor_tensor(q_fade[:, m0.par].rearrange("p g t -> p (g t)"), ps_t[:, 0:2 * P],
                                      fade_q[:, :, :].rearrange("p g t -> p (g t)"), ALU.mult)\
                       .then_inc(s["qfade_done"], 1)
                if m2.live:
                    dve.wait_ge(s["y_done"], m2.n + 1)
                    dve.wait_ge(xk_in[m2.c], (m2.b + 1) * 16)
                    dve.tensor_tensor(z[:, m2.par, :], ps_y[:, 0:D], x_tok[:, m2.c, :], ALU.add)\
                       .then_inc(s["z_done"], 1)
                if m1.live:
                    dve.wait_ge(s["srstd_done"], m1.n + 1)
                    need(dve, s["gated_done"], m1.n)
                    dve.tensor_tensor(normed[:, :].rearrange("p (h c) -> p h c", h=NH),
                                      ps_o[:, :].rearrange("p (h c) -> p h c", h=NH),
                                      srstd[:, m1.par, :].unsqueeze(2).to_broadcast([P, NH, DV]), ALU.mult)\
                       .then_inc(s["normed_done"], 1)
                    dve.wait_ge(s["normed_done"], m1.n + 1)
                    dve.wait_ge(s["gate_done"], m1.n + 1)
                    need(dve, s["n_done"], m1.n - 1)
                    dve.tensor_tensor(gated[:, m1.par, :], normed[:, :], gate[:, m1.par, :], ALU.mult)\
                       .then_inc(s["gated_done"], 1)
                if m4.live:
                    dve.wait_ge(s["c_done"], m4.n + 1)
                    need(dve, s["count_done"], m4.n)
                    dve.tensor_tensor(place[:, :], ps_y[:, 384:400], count[:, :], ALU.add).then_inc(s["place_sum"], 1)
                    dve.wait_ge(s["place_sum"], m4.n + 1)
                    dve.tensor_tensor(count[:, :], ps_y[:, 400:416], count[:, :], ALU.add).then_inc(s["count_done"], 1)
                    dve.tensor_tensor(place[:, :], place[:, :], hot[:, :], ALU.mult).then_inc(s["place_mul"], 1)
                    dve.wait_ge(s["place_mul"], m4.n + 1)
                    dve.tensor_reduce(pick[:, m4.par, 2:4], place[:, :].rearrange("p (j e) -> p j e", e=E), AX,
                                      ALU.add).then_inc(s["place_done"], 1)
                    hold(dve, s["place_done"], m4.n + 1, s["dve_held"])
                    dve.tensor_copy(pick_all[:, bass.ds(m4.n, 1), :].rearrange("p a j -> p (a j)"), pick[:, m4.par, :])
                if m2.live:
                    dve.wait_ge(s["z_done"], m2.n + 1)
                    dve.bn_stats(zstat[:, m2.par, :], z[:, m2.par, :]).then_inc(s["zstat_done"], 1)
                    hold(dve, s["zstat_done"], m2.n + 1, s["dve_held"])
                    dve.bn_aggr(zmean[:, m2.par, :], zstat[:, m2.par, :]).then_inc(s["zmean_done"], 1)
                if m0.live:
                    dve.wait_ge(s["s_done"], m0.n + 1)
                    need(dve, s["o_done"], m0.n - 1)
                    dve.tensor_tensor(probs[:, m0.par].rearrange("p h t -> p (h t)"), ps_s[:, :],
                                      fade[:, :, :].rearrange("p h t -> p (h t)"), ALU.mult)\
                       .then_inc(s["probs_done"], 1)
                if m0.live and m0.c < NC - 1:
                    dve.wait_ge(s["u_done"], m0.b * (NC - 1) + m0.c + 1)
                    need(dve, s["o_done"], m0.n)
                    if m0.c > 0:
                        dve.wait_ge(s["state_done"], m0.b * (NC - 1) + m0.c)
                    new, old = state[:, 1 - m0.par], state[:, m0.par]
                    for j in range(4):
                        r, col = slice(DK * j, DK * j + DK), slice(DV * j, DV * j + DV)
                        part = ps_v[r, :].rearrange("p (g c) -> p g c", g=2)[:, :, col]
                        if m0.c == 0:
                            o = dve.tensor_copy(new[r, :, col], part)
                        else:
                            for g in range(2):
                                o = dve.scalar_tensor_tensor(new[r, g, col], old[r, g, col], fade_c[r, g:g + 1],
                                                             part[:, g, :], ALU.mult, ALU.add)
                    o.then_inc(s["state_done"], 1)

            steps(dve, step)

        @block.gpsimd
        def _(pool):
            pool.memset(zeros[:, :], float(TOPK * N)).then_inc(s["zero_set"], 1)
            pool.memset(half_neg[:, :], -0.5).then_inc(s["zero_set"], 1)
            pool.memset(q_diag[:, :, :, :, :], 0.0).then_inc(s["small_set"], 1)
            pool.memset(v_pad[:, :, :, :], 0.0).then_inc(s["small_set"], 1)
            pool.memset(state[:, :, :, :], 0.0).then_inc(s["small_set"], 1)
            pool.wait_ge(s["const_in"], 16)
            pool.wait_ge(s["zero_set"], 2)
            pool.tensor_copy(token[:, :, :], token0).then_inc(s["zero_set"], 1)

            def split_weights(j):
                raw, high, low = parts[j]
                pool.wait_ge(w_hi_done[j], 1)
                pool.tensor_tensor(low, raw, high.bitcast(F32), ALU.subtract).then_inc(w_lo_done[j], 1)

            split_weights(2)

            def split_x(m):
                pool.wait_ge(s["xhi_done"], m.n + 1)
                pool.tensor_tensor(xt_lo[:, m.c], xt_raw[:, m.c], xt_hi[:, m.c].bitcast(F32), ALU.subtract)\
                    .then_inc(s["xlo_done"], 1)

            def rotated_sum(m):
                need(pool, s["t_done"], m.n - 1)
                pool.wait_ge(s["rotated"], 2 * m.n + 2)
                pool.tensor_tensor(qk[:, m.par, :], rot_a[:, :], rot_b[:, :], ALU.add).then_inc(s["qk_sum"], 1)

            def scatter_ids(m):
                hold(pool, s["token_set"], m.n + 1, s["pool_held"])
                hold(pool, s["slot_done"], m.n + 1, s["pool_held"])
                for j in range(TOPK):
                    pool.indirect_dma_start(slot_ids, bass.IndirectOffsetOnAxis(ap=slot[:, m.par, j:j + 1], axis=0),
                                            token[:, m.c, j:j + 1], None, bounds_check=TOPK * SLOTS - 1,
                                            oob_is_err=False).then_inc(ids_sent[m.c], 16)

            rotated_sum(Chunk(0, 0))

            def step(b, c):
                m0, m1, m2, m3, m4 = (Chunk(b, c, lag) for lag in range(5))
                if m1.live:
                    hold(pool, s["ssum_done"], m1.n + 1, s["pool_held"])
                    pool.tensor_scalar(svar[:, :], ssum[:, m1.par, :], 1.0 / DV, EPS, ALU.mult, ALU.add)\
                        .then_inc(s["svar_done"], 1)
                    need(pool, s["normed_done"], m1.n - 1)
                    pool.wait_ge(s["svar_done"], m1.n + 1)
                    pool.tensor_tensor(srstd[:, m1.par, :], svar[:, :], half_neg[:, :], ALU.pow)\
                        .then_inc(s["srstd_done"], 1)
                if m1.live and Chunk(b + 1, c, 1).live:
                    split_x(Chunk(b + 1, c, 1))
                if m0.live and m0.c < NC - 1:
                    if isinstance(m0.n, int) and m0.n == 0:
                        pool.wait_ge(s["fade_set"], 1)
                    need(pool, s["u_done"], m0.b * (NC - 1) + max(m0.c - 1, 0))
                    pool.wait_ge(s["qk_sum"], m0.n + 1)
                    pool.tensor_tensor(k_fade[:, m0.par].rearrange("p (h c) -> p h c", h=NH),
                                       qk[:, m0.par, D:2 * D].rearrange("p (h c) -> p h c", h=NH),
                                       fade_k.to_broadcast([P, NH, DK]), ALU.mult)\
                        .then_inc(s["kfade_done"], 1)
                if Chunk(b, c, 5).live:
                    scatter_ids(Chunk(b, c, 5))
                if m2.live:
                    hold(pool, s["zmean_done"], m2.n + 1, s["pool_held"])
                    pool.tensor_scalar(zvar[:, :], zmean[:, m2.par, 1:2], EPS, None, ALU.add)\
                        .then_inc(s["zvar_done"], 1)
                    need(pool, s["x1_done"], m2.n - 1)
                    pool.wait_ge(s["zvar_done"], m2.n + 1)
                    pool.tensor_tensor(zrstd[:, m2.par, :], zvar[:, :], half_neg[:, 0:1], ALU.pow)\
                        .then_inc(s["zrstd_done"], 1)
                if isinstance(m0.n, int) and m0.n == 0:
                    split_weights(3)
                    pool.wait_ge(s["zero_set"], 3)
                    pool.wait_ge(s["ids_set"], 16)
                    pool.memset(zeros[:, :], 0.0).then_inc(s["zero_set"], 1)
                if m4.live:
                    hold(pool, s["place_done"], m4.n + 1, s["pool_held"])
                    at = m4.n * 6
                    pool.tensor_scalar(over[:, :], pick[:, m4.par, 2:4], float(CAP), SKIP, ALU.is_ge, ALU.mult)\
                        .then_inc(s["slot_step"], 1)
                    pool.tensor_scalar(sbase[:, :], pick[:, m4.par, 0:2], float(CAP), None, ALU.mult)\
                        .then_inc(s["slot_step"], 1)
                    pool.tensor_tensor(splace[:, :], pick[:, m4.par, 2:4], sign2, ALU.mult).then_inc(s["slot_step"], 1)
                    pool.wait_ge(s["slot_step"], at + 2)
                    pool.tensor_tensor(sbase[:, :], sbase[:, :], off2, ALU.add).then_inc(s["slot_step"], 1)
                    pool.wait_ge(s["slot_step"], at + 3)
                    pool.tensor_tensor(splace[:, :], splace[:, :], over[:, :], ALU.add).then_inc(s["slot_step"], 1)
                    pool.wait_ge(s["slot_step"], at + 5)
                    pool.tensor_tensor(slot_f[:, :], sbase[:, :], splace[:, :], ALU.add).then_inc(s["slot_step"], 1)
                    need(pool, ids_sent[(m4.c + 2) % NC], (m4.b + m4.c // 2) * 32)
                    hold(pool, s["slot_step"], at + 6, s["pool_held"])
                    pool.tensor_copy(slot[:, m4.par, :], slot_f[:, :]).then_inc(s["slot_done"], 1)
                    hold(pool, ids_sent[m4.c], m4.b * 32, s["pool_held"])
                    pool.tensor_scalar(token[:, m4.c, :], token[:, m4.c, :], float(T), None, ALU.add)\
                        .then_inc(s["token_set"], 1)
                if Chunk(b, c, -1).live:
                    rotated_sum(Chunk(b, c, -1))

            steps(pool, step)
            scatter_ids(Chunk(B - 1, NC - 1))
            for k in range(NC):
                pool.wait_ge(ids_sent[k], 32 * B)
            pool.wait_ge(s["y_zeroed"], 16 * 2 * B)


def phase_two(nc, sem, v):
    w1T, b1, w2, b2, out = (v[k] for k in ("w1T", "b1", "w2", "b2", "out"))
    x1_rows, slot_ids, y_rows = (v[k] for k in ("x1_rows", "slot_ids", "y_rows"))
    x1_all, top_all, pick_all, count = (v[k] for k in ("x1_all", "top_all", "pick_all", "count"))
    landing, w1_raw, w2_raw, expert_in = (v[k] for k in ("landing", "w1_raw", "w2_raw", "expert_in"))
    ident, iota8, slot_no = (v[k] for k in ("ident", "iota8", "slot_no"))
    UE = UNITS // E
    PAIR = 2 * UE
    GROUP = 2
    BUFS = 4
    LAPS = TILES // GROUP // BUFS

    with ExitStack() as ctx:
        def sb(name, shape, dt=F32):
            return ctx.enter_context(nc.sbuf_tensor(name, shape, dt))

        def psum(name, shape):
            return ctx.enter_context(nc.psum_tensor(name, shape, F32))

        ys = landing[:, 0:BUFS * TOPK * GROUP * D].rearrange("p (b j a d) -> p b j a d", b=BUFS, j=TOPK, a=GROUP)
        w1_hi, w1_lo = (sb(f"w1_{x}", [P, 2, KD, H], F32R) for x in ("hi", "lo"))
        w2_hi, w2_lo = (sb(f"w2_{x}", [P, 2, HB, D], F32R) for x in ("hi", "lo"))
        b1_all = sb("b1_all", [P, E, HB])
        b2_all = sb("b2_all", [P, E, D])
        rows_in = sb("rows_in", [P, 2, UM, D])
        xg_hi, xg_lo = (sb(f"xg_{x}", [P, 2, KD, UT], F32R) for x in ("hi", "lo"))
        hidden = sb("hidden", [P, 2, UT])
        h_hi, h_lo = (sb(f"h_{x}", [P, 4, UT], F32R) for x in ("hi", "lo"))
        rows_out = sb("rows_out", [P, 2, UM, D])
        ids = sb("ids", [P, P])
        ids_t = sb("ids_t", [P, TOPK, SLOTS // P])
        firsts = sb("firsts", [P, SLOTS // P])
        diff = sb("diff", [P, SLOTS // P])
        dest = sb("dest", [P, SLOTS // P], I32)
        source = sb("source", [P, SLOTS // P], I32)
        dest_u = sb("dest_u", [P, 2, UM], I32)
        source_u = sb("source_u", [P, 2, UM], I32)
        share = sb("share", [P, TOPK, TILES])
        lead = sb("lead", [P, TILES])
        spread = sb("spread", [P, TILES])
        second = sb("second", [P, TILES, E])
        second_n = sb("second_n", [P, TILES, E])
        filled = sb("filled", [P, TILES])
        valid = sb("valid", [P, TOPK, TILES])
        fin = sb("fin", [P, BUFS, GROUP, D])
        fstat = sb("fstat", [P, BUFS, GROUP, 6])
        fmean = sb("fmean", [P, BUFS, GROUP, 2])
        fvar = sb("fvar", [P, BUFS, GROUP])
        frstd = sb("frstd", [P, BUFS, GROUP])
        fshift = sb("fshift", [P, BUFS, GROUP])
        share_diag = sb("share_diag", [P, TILES // GROUP, TOPK, P])
        minus_half = sb("minus_half", [P, GROUP])

        ps_h = [psum(f"ps_h{i}", [P, UT]) for i in range(2)]
        ps_x = psum("ps_x", [P, KD * UT])
        ps_out = [psum(f"ps_out{i}", [P, UM * D]) for i in range(2)]
        ps_fin = [ps_h[0], ps_h[1], ps_x[:, 0:UT], ps_x[:, UT:2 * UT]]

        names = """bias_in ids_in ids_turned ids_out setup_step source_set
        turned xhi xlo fc1_done relu_done hhi_done hlo_done fc2_half fc2_done whi_done wlo_done
        picked_in picked_out act_held dve_held2 pool_held2
        spread_set lead_set share_done diag_set mixed
        ys_first ys_sum fstat_done fmean_done half_set fstep frstd_done fshift_done fin_done""".split()
        s = {k: sem(k + "_2") for k in names}
        rows_done = [sem(f"rows_done{i}") for i in range(2)]
        gathered = [sem(f"gathered{i}") for i in range(2)]
        scattered = [sem(f"scattered{i}") for i in range(2)]
        ys_in = [sem(f"ys_in{i}") for i in range(BUFS)]
        stored = [sem(f"stored{i}") for i in range(BUFS)]

        block = ctx.enter_context(nc.Block())

        def pairs(eng, unit):
            for q in range(PAIR):
                unit(0, q, False)
            with eng.Fori(1, E // 2 - 1) as i:
                for q in range(PAIR):
                    unit(i, q, False)
            for q in range(PAIR):
                unit(E // 2 - 1, q, True)

        def laps(eng, group):
            for k in range(BUFS):
                group(0, k)
            with eng.Fori(1, LAPS) as i:
                for k in range(BUFS):
                    group(i, k)

        @block.sync
        def _(sp):
            sp.dma_start(ids[:, :], slot_ids.rearrange("(c p) o -> c (p o)", p=P)).then_inc(s["ids_in"], 16)
            sp.dma_start(b1_all[:, :, :], b1).then_inc(s["bias_in"], 16)
            sp.dma_start(b2_all[:, :, :], bass.AP(b2.tensor, 0, [[0, P], [D, E], [1, D]])).then_inc(s["bias_in"], 16)
            with sp.Fori(1, E) as e:
                sp.wait_ge(s["wlo_done"], e * HB)
                for raw, w in ((w1_raw, w1T), (w2_raw, w2)):
                    sp.dma_start(raw[:, :, :], w[bass.ds(e, 1)].rearrange("e p k n -> p (e k) n"))\
                      .then_inc(expert_in, 16)
            for i in range(2):
                sp.wait_ge(scattered[i], 16 * UM * UNITS // 2)

            def load(i, k):
                g = i * BUFS + k
                need(sp, s["ys_sum"], g - BUFS + 1)
                need(sp, s["mixed"], g - BUFS + 1)
                for j in range(TOPK):
                    src = y_rows[bass.ds(g * (GROUP * P) + j * N, GROUP * P), :].rearrange("(a p) d -> p a d", p=P)
                    sp.dma_start(ys[:, k, j], src).then_inc(ys_in[k], 16)

            laps(sp, load)
            for k in range(BUFS):
                sp.wait_ge(stored[k], 16 * LAPS)

        @block.scalar
        def _(act):
            def weights(e, par, piece):
                act.wait_ge(expert_in, 32 * (e + 1))
                need(act, s["fc2_done"], (e - 1) * HB * UE)
                c = slice(P * piece, P * piece + P)
                act.activation(w1_hi[:, par, :, c], w1_raw[:, :, c], ACT.Copy)
                act.activation(w2_hi[:, par, piece, :], w2_raw[:, piece, :], ACT.Copy).then_inc(s["whi_done"], 1)

            def turned(u, par):
                need(act, s["fc1_done"], (u - 1) * HB)
                for k in range(KD):
                    act.wait_ge(s["turned"], KD * u + k + 1)
                    act.activation(xg_hi[:, par, k, :], ps_x[:, UT * k:UT * k + UT], ACT.Copy).then_inc(s["xhi"], 1)

            def relu(e, u, k):
                g = u * HB + k
                need(act, s["hlo_done"], g - 1)
                hold(act, s["fc1_done"], g + 1, s["act_held"])
                act.activation(hidden[:, k % 2, :], ps_h[k % 2][:, :], ACT.Relu,
                               bias=b1_all[:, bass.ds(e, 1), k:k + 1].rearrange("p a b -> p (a b)"))\
                   .then_inc(s["relu_done"], 1)

            for piece in range(HB):
                weights(0, 0, piece)
            turned(0, 0)
            act.wait_ge(s["spread_set"], 1)
            act.activation(lead[:, :], spread[:, :], ACT.Tanh, scale=0.5).then_inc(s["lead_set"], 1)
            act.wait_ge(s["bias_in"], 32)
            for k in range(2):
                relu(0, 0, k)

            def unit(i, q, last):
                u, e = i * PAIR + q, i * 2 + q // UE
                for k in range(2, HB + 2):
                    if k < HB:
                        relu(e, u, k)
                    elif not (last and q == PAIR - 1):
                        relu(i * 2 + (q + 1) // UE, u + 1, k - HB)
                    if k == 6 and not (last and q == PAIR - 1):
                        turned(u + 1, (q + 1) % 2)
                    if q % UE == 0 and not (last and q == UE):
                        weights(e + 1, (q // UE + 1) % 2, k - 2)
                if isinstance(u, int) and u == 0:
                    act.wait_ge(s["share_done"], 1)
                for j in range(TOPK):
                    o = act.activation(share_diag[:, bass.ds(u, 1), j, :].rearrange("p a d -> p (a d)"), ident,
                                       ACT.Copy, scale=share[:, j, bass.ds(u * GROUP + 1, 1)])
                o.then_inc(s["diag_set"], 1)

            pairs(act, unit)

            def normalise(i, k):
                g = i * BUFS + k
                act.wait_ge(s["fshift_done"], g + 1)
                for a, rows in ((0, fin[:, k, 0, :]), (1, ps_fin[k][:, 0:D])):
                    act.activation(fin[:, k, a, :], rows, ACT.Identity, bias=fshift[:, k, a:a + 1],
                                   scale=frstd[:, k, a:a + 1]).then_inc(s["fin_done"], 1)
                act.wait_ge(s["fin_done"], GROUP * (g + 1))
                act.dma_start(out[bass.ds(g * (GROUP * P), GROUP * P), :].rearrange("(a p) d -> p a d", p=P),
                              fin[:, k]).then_inc(stored[k], 16)

            laps(act, normalise)

        @block.tensor
        def _(pe):
            def three(out_, a_hi, a_lo, b_hi, b_lo, last, first):
                pe.matmul(out_, a_hi, b_hi, start=first, stop=False, skip_group_check=True)
                pe.matmul(out_, a_hi, b_lo, start=False, stop=False, skip_group_check=True)
                return pe.matmul(out_, a_lo, b_hi, start=False, stop=last, skip_group_check=True)

            def turn(u, par, nth):
                pe.wait_ge(gathered[par], 16 * UM * nth)
                need(pe, s["xlo"], KD * u)
                for k in range(KD):
                    for m in range(UM):
                        o = pe.transpose(ps_x[:, UT * k + P * m:UT * k + P * m + P],
                                         rows_in[:, par, m, P * k:P * k + P], ident)
                    o.then_inc(s["turned"], 1)

            def fc1(e, u, par, ue, k):
                g = u * HB + k
                if k == 0 and ue == 0:
                    pe.wait_ge(s["wlo_done"], (e + 1) * HB)
                need(pe, s["relu_done"], g - 1)
                c = slice(P * k, P * k + P)
                for d in range(KD):
                    if k == 0:
                        pe.wait_ge(s["xlo"], KD * u + d + 1)
                    o = three(ps_h[k % 2][:, :], w1_hi[:, par, d, c], w1_lo[:, par, d, c],
                              xg_hi[:, ue, d, :], xg_lo[:, ue, d, :], d == KD - 1, d == 0)
                o.then_inc(s["fc1_done"], 1)

            def fc2(e, u, par, ue, k, before):
                g = u * HB + k
                pe.wait_ge(s["hlo_done"], g + 1)
                if k == 0:
                    need(pe, rows_done[ue], 2 * before)
                for m in range(UM):
                    c = slice(P * m, P * m + P)
                    o = three(ps_out[ue][:, D * m:D * m + D], h_hi[:, k % 4, c], h_lo[:, k % 4, c],
                              w2_hi[:, par, k, :], w2_lo[:, par, k, :], k == HB - 1, k == 0 and m % 2 == 0)
                    if k == HB - 1 and m == UM // 2 - 1:
                        o.then_inc(s["fc2_half"], 1)
                o.then_inc(s["fc2_done"], 1)

            pe.wait_ge(s["ids_in"], 16)
            pe.transpose(ps_h[0][:, 0:P], ids[:, :], ident).then_inc(s["ids_turned"], 1)
            turn(0, 0, 1)
            pe.wait_ge(s["ids_out"], 1)
            for k in range(2):
                fc1(0, 0, 0, 0, k)

            def unit(i, q, last):
                u = i * PAIR + q
                for k in range(2, HB + 2):
                    if k < HB:
                        fc1(i * 2 + q // UE, u, q // UE, q % 2, k)
                    elif not (last and q == PAIR - 1):
                        fc1(i * 2 + (q + 1) // UE, u + 1, (q + 1) // UE % 2, (q + 1) % 2, k - HB)
                    fc2(i * 2 + q // UE, u, q // UE, q % 2, k - 2, i * (PAIR // 2) + q // 2)
                    if k == 6 and not (last and q == PAIR - 1):
                        turn(u + 1, (q + 1) % 2, i * (PAIR // 2) + (q + 1) // 2 + 1)

            pairs(pe, unit)

            pe.wait_ge(s["diag_set"], TILES // GROUP)
            for g in range(TILES // GROUP):
                k = g % BUFS
                need(pe, s["fin_done"], GROUP * (g - BUFS + 1))
                pe.wait_ge(ys_in[k], (g // BUFS + 1) * 16 * TOPK)
                pe.matmul(ps_fin[k][:, 0:D], ident, x1_all[:, g * GROUP + 1, :], start=True, stop=False)
                for j in range(TOPK):
                    o = pe.matmul(ps_fin[k][:, 0:D], share_diag[:, g, j, :], ys[:, k, j, 1, :],
                                  start=False, stop=j == TOPK - 1)
                o.then_inc(s["mixed"], 1)

        @block.vector
        def _(dve):
            def weights(e, par, piece):
                dve.wait_ge(s["whi_done"], e * HB + piece + 1)
                c = slice(P * piece, P * piece + P)
                dve.tensor_tensor(w1_lo[:, par, :, c], w1_raw[:, :, c], w1_hi[:, par, :, c].bitcast(F32), ALU.subtract)
                dve.tensor_tensor(w2_lo[:, par, piece, :], w2_raw[:, piece, :], w2_hi[:, par, piece, :].bitcast(F32),
                                  ALU.subtract).then_inc(s["wlo_done"], 1)

            def turned(u, par):
                for k in range(KD):
                    dve.wait_ge(s["xhi"], KD * u + k + 1)
                    dve.tensor_tensor(xg_lo[:, par, k, :], ps_x[:, UT * k:UT * k + UT],
                                      xg_hi[:, par, k, :].bitcast(F32), ALU.subtract).then_inc(s["xlo"], 1)

            def split(u, k):
                g = u * HB + k
                dve.wait_ge(s["relu_done"], g + 1)
                need(dve, s["fc2_done"], g - 2)
                dve.tensor_copy(h_hi[:, k % 4, :], hidden[:, k % 2, :]).then_inc(s["hhi_done"], 1)
                dve.wait_ge(s["hhi_done"], g + 1)
                dve.tensor_tensor(h_lo[:, k % 4, :], hidden[:, k % 2, :], h_hi[:, k % 4, :].bitcast(F32), ALU.subtract)\
                   .then_inc(s["hlo_done"], 1)

            passed = [0]

            def chain(instruction):
                instruction.then_inc(s["setup_step"], 1)
                passed[0] += 1
                dve.wait_ge(s["setup_step"], passed[0])

            chain(dve.tensor_tensor(firsts[:, :].rearrange("p (e k) -> p e k", e=E), slot_no,
                                    count[:, 0:E].unsqueeze(2).to_broadcast([P, E, CAP // P]), ALU.is_lt))
            dve.wait_ge(s["ids_turned"], 1)
            dve.tensor_copy(ids_t[:, :, :].rearrange("p j c -> p (j c)"), ps_h[0][:, 0:P]).then_inc(s["ids_out"], 1)
            dve.wait_ge(s["ids_out"], 1)
            chain(dve.tensor_tensor(diff[:, :], ids_t[:, 0, :], ids_t[:, 1, :], ALU.subtract))
            chain(dve.tensor_tensor(diff[:, :], diff[:, :], firsts[:, :], ALU.mult))
            chain(dve.tensor_tensor(dest[:, :], diff[:, :], ids_t[:, 1, :], ALU.add))
            dve.tensor_scalar(source[:, :], dest[:, :], N - 1, None, ALU.bitwise_and).then_inc(s["source_set"], 1)
            dve.tensor_tensor(spread[:, :], top_all[:, :, 0], top_all[:, :, 1], ALU.subtract)\
               .then_inc(s["spread_set"], 1)
            for piece in range(HB):
                weights(0, 0, piece)
            turned(0, 0)
            for k in range(2):
                split(0, k)
            chain(dve.tensor_tensor(second[:, :, :], iota8[:, 0:1, :].to_broadcast([P, TILES, E]),
                                    pick_all[:, :, 1:2].to_broadcast([P, TILES, E]), ALU.is_equal))
            chain(dve.tensor_tensor(second_n[:, :, :], second[:, :, :],
                                    count[:, 0:E].unsqueeze(1).to_broadcast([P, TILES, E]), ALU.mult))
            chain(dve.tensor_reduce(filled[:, :], second_n[:, :, :], AX, ALU.add))
            chain(dve.tensor_tensor(filled[:, :], filled[:, :], pick_all[:, :, 3], ALU.add))
            chain(dve.tensor_scalar(valid[:, 0, :], pick_all[:, :, 2], float(CAP), None, ALU.is_lt))
            chain(dve.tensor_scalar(valid[:, 1, :], filled[:, :], float(CAP), None, ALU.is_lt))
            dve.wait_ge(s["lead_set"], 1)
            for j in range(TOPK):
                chain(dve.tensor_scalar(share[:, j, :], lead[:, :], 0.5 - j, 0.5, ALU.mult, ALU.add))
            dve.tensor_tensor(share[:, :, :], share[:, :, :], valid[:, :, :], ALU.mult).then_inc(s["share_done"], 1)
            dve.wait_ge(s["bias_in"], 32)

            def unit(i, q, last):
                u = i * PAIR + q
                for k in range(2, HB + 2):
                    if k < HB:
                        split(u, k)
                    elif not (last and q == PAIR - 1):
                        split(u + 1, k - HB)
                    if k == 6 and not (last and q == PAIR - 1):
                        turned(u + 1, (q + 1) % 2)
                    if q % UE == 0 and not (last and q == UE):
                        weights(i * 2 + q // UE + 1, (q // UE + 1) % 2, k - 2)
                need(dve, scattered[q % 2], (i * (PAIR // 2) + q // 2) * 16 * UM)
                bias = b2_all[:, bass.ds(i * 2 + q // UE, 1), :].to_broadcast([P, 2, D])
                for m in range(0, UM, 2):
                    if m == 0:
                        dve.wait_ge(s["fc2_half"], u + 1)
                    else:
                        dve.wait_ge(s["fc2_done"], (u + 1) * HB)
                    dve.tensor_tensor(rows_out[:, q % 2, m:m + 2, :],
                                      ps_out[q % 2][:, D * m:D * m + 2 * D].rearrange("p (m d) -> p m d", m=2),
                                      bias, ALU.add).then_inc(rows_done[q % 2], 1)

            pairs(dve, unit)

            def group(i, k):
                g = i * BUFS + k
                dve.wait_ge(s["share_done"], 1)
                need(dve, stored[k], i * 16)
                dve.wait_ge(ys_in[k], (i + 1) * 16 * TOPK)
                tile = bass.ds(g * GROUP, 1)
                dve.scalar_tensor_tensor(ys[:, k, 0, 0, :], ys[:, k, 0, 0, :], share[:, 0, tile],
                                         x1_all[:, tile, :].rearrange("p a d -> p (a d)"),
                                         ALU.mult, ALU.add).then_inc(s["ys_first"], 1)
                dve.wait_ge(s["ys_first"], g + 1)
                dve.scalar_tensor_tensor(fin[:, k, 0, :], ys[:, k, 1, 0, :], share[:, 1, tile], ys[:, k, 0, 0, :],
                                         ALU.mult, ALU.add).then_inc(s["ys_sum"], 1)
                dve.wait_ge(s["mixed"], g + 1)
                dve.bn_stats(fstat[:, k, 1, :], ps_fin[k][:, 0:D]).then_inc(s["fstat_done"], 1)
                dve.wait_ge(s["ys_sum"], g + 1)
                dve.bn_stats(fstat[:, k, 0, :], fin[:, k, 0, :]).then_inc(s["fstat_done"], 1)
                for n, a in enumerate((1, 0)):
                    hold(dve, s["fstat_done"], GROUP * g + n + 1, s["dve_held2"])
                    dve.bn_aggr(fmean[:, k, a, :], fstat[:, k, a, :]).then_inc(s["fmean_done"], 1)

            laps(dve, group)

        @block.gpsimd
        def _(pool):
            def gather(u, par):
                hold(pool, s["turned"], KD * (u - 1), s["pool_held2"])
                pool.tensor_copy(source_u[:, par, :], source[:, bass.ds(u * UM, UM)]).then_inc(s["picked_in"], 1)
                hold(pool, s["picked_in"], u + 1, s["pool_held2"])
                for m in range(UM):
                    pool.indirect_dma_start(rows_in[:, par, m, :], None, x1_rows,
                                            bass.IndirectOffsetOnAxis(ap=source_u[:, par, m:m + 1], axis=0))\
                        .then_inc(gathered[par], 16)

            def scatter(u, par, nth):
                hold(pool, scattered[par], nth * 16 * UM, s["pool_held2"])
                pool.tensor_copy(dest_u[:, par, :], dest[:, bass.ds(u * UM, UM)]).then_inc(s["picked_out"], 1)
                hold(pool, s["picked_out"], u + 1, s["pool_held2"])
                for m in range(UM):
                    if m % 2 == 0:
                        hold(pool, rows_done[par], 2 * nth + m // 2 + 1, s["pool_held2"])
                    pool.indirect_dma_start(y_rows, bass.IndirectOffsetOnAxis(ap=dest_u[:, par, m:m + 1], axis=0),
                                            rows_out[:, par, m, :], None, bounds_check=TOPK * N - 1, oob_is_err=False)\
                        .then_inc(scattered[par], 16)

            pool.memset(minus_half[:, :], -0.5).then_inc(s["half_set"], 1)
            pool.wait_ge(s["half_set"], 1)
            pool.wait_ge(s["source_set"], 1)
            gather(0, 0)
            gather(1, 1)

            def unit(i, q, last):
                u = i * PAIR + q
                scatter(u, q % 2, i * (PAIR // 2) + q // 2)
                if not (last and q >= PAIR - 2):
                    gather(u + 2, q % 2)

            pairs(pool, unit)

            def root(i, k):
                g = i * BUFS + k
                hold(pool, s["fmean_done"], GROUP * (g + 1), s["pool_held2"])
                pool.tensor_scalar(fvar[:, k, :], fmean[:, k, :, 1], EPS, None, ALU.add).then_inc(s["fstep"], 1)
                pool.tensor_scalar(fshift[:, k, :], fmean[:, k, :, 0], -1.0, None, ALU.mult).then_inc(s["fstep"], 1)
                pool.wait_ge(s["fstep"], 2 * g + 1)
                pool.tensor_tensor(frstd[:, k, :], fvar[:, k, :], minus_half[:, :], ALU.pow)\
                    .then_inc(s["frstd_done"], 1)
                pool.wait_ge(s["fstep"], 2 * g + 2)
                pool.wait_ge(s["frstd_done"], g + 1)
                pool.tensor_tensor(fshift[:, k, :], fshift[:, k, :], frstd[:, k, :], ALU.mult)\
                    .then_inc(s["fshift_done"], 1)

            laps(pool, root)


def _tables():
    f = np.float32
    pos = np.arange(T, dtype=f)
    freq = f(1) / (10000.0 ** (np.arange(D // 2) / (D // 2))).astype(f)
    phase = (pos[:, None] * freq[None, :]).astype(np.float64)
    width = ((np.arange(0, D, 2) + 0.4 * D) / (1.4 * D)).astype(f).astype(np.float64)
    grow = width[None, :] ** (pos[:, None].astype(np.float64) / 512.0)
    rope = np.zeros((2, T, 2, D), np.float64)
    for i, scale in enumerate((grow * DK ** -0.5, 1.0 / grow)):
        rope[0, :, i, :] = np.repeat(np.cos(phase) * scale, 2, axis=1)
        rope[1, :, i, 0::2] = -np.sin(phase) * scale
        rope[1, :, i, 1::2] = np.sin(phase) * scale
    rope = rope.reshape(2, NC, P, 2 * D).transpose(0, 2, 1, 3).astype(f)
    p = np.arange(P)
    token = [[[j * N + c * P - T for j in range(TOPK)] for c in range(NC)]]
    parts = [
        np.eye(P),
        (p[:, None] < p[None, :]),
        np.tile(np.arange(E), (P, TOPK)),
        np.tile([1, -1], (P, 1)),
        np.tile([0, SLOTS + CAP - 1], (P, 1)),
        (np.array(token) + p[:, None, None]).reshape(P, NC * TOPK),
        np.tile(np.arange(CAP // P) * P, (P, E)) + p[:, None],
    ]
    return np.ascontiguousarray(rope), np.concatenate(parts, axis=1).astype(f)


def kernel(**inputs):
    import numpy as _np
    import concourse.bacc as _bacc
    from concourse import mybir as _mybir
    from concourse.bass_utils import run_bass_kernel_spmd as _run

    x, w_qkv, w_gated, w_proj, decay, gate_w, w1, b1, w2, b2 = (
        _np.asarray(inputs[k]) for k in (
            "L0_attn_hidden_states", "L0_attn_w_qkv", "L0_attn_w_gated", "L0_attn_w_proj", "L0_attn_decay",
            "L0_ffn_gate_w", "L0_ffn_fc1_w", "L0_ffn_fc1_b", "L0_ffn_fc2_w", "L0_ffn_fc2_b"))
    rows = x.reshape(N, D)
    rope, consts = _tables()
    arrays = {
        "xT": rows.T.reshape(KD, P, N).transpose(1, 0, 2),
        "xk": rows,
        "wT": _np.concatenate([w_qkv, w_gated], axis=0).T.reshape(KD, P, -1).transpose(1, 0, 2),
        "wpT": w_proj.T.reshape(VD // P, P, D).transpose(1, 0, 2),
        "decay": decay.reshape(NH, 1),
        "gwT": gate_w.T.reshape(KD, P, E).transpose(1, 0, 2),
        "w1T": w1.transpose(0, 2, 1).reshape(E, KD, P, H).transpose(0, 2, 1, 3),
        "b1": b1.reshape(E, HB, P).transpose(2, 0, 1),
        "w2": w2.reshape(E, HB, P, D).transpose(0, 2, 1, 3),
        "b2": b2.reshape(E, D),
        "rope": rope,
        "consts": consts,
    }
    arrays = {f"in_{k}": _np.ascontiguousarray(a) for k, a in arrays.items()}
    nc = _bacc.Bacc("TRN2", target_bir_lowering=False, num_devices=1)
    args = [nc.dram_tensor(k, a.shape, _mybir.dt.from_np(a.dtype), kind="ExternalInput").ap()
            for k, a in arrays.items()]
    args.append(nc.dram_tensor("out_0", (N, D), F32, kind="ExternalOutput").ap())
    moe_layer(nc, *args)
    r = _run(nc, [arrays], core_ids=[0])
    return r.results[0]["out_0"].reshape(B, T, D)
```
